# Optimizing a Trainium2 kernel written in Bass

```python
import numpy as np
import jax
import jax.numpy as jnp

def _softmax(x, axis=-1):
    return jax.nn.softmax(x, axis=axis)

def _gelu(x):
    return jax.nn.gelu(x, approximate=True)

def _silu(x):
    return jax.nn.silu(x)

def _sigmoid(x):
    return jax.nn.sigmoid(x)

def _layernorm(x, axis=-1, eps=1e-05):
    m = jnp.mean(x, axis=axis, keepdims=True)
    v = jnp.var(x, axis=axis, keepdims=True)
    return (x - m) / jnp.sqrt(v + eps)

def _scatter_add(tgt, idx, src, axis=0):
    return tgt.at[idx].add(src)

def _segment_sum(src, seg, n):
    return jax.ops.segment_sum(src, seg, n)
kernel_name = 'mk_seq_postln_d1_jaxref_r8_41e9c8'

def setup_inputs(seed: int=0):
    np.random.seed(seed)
    _w = jnp.asarray

    def _L0_attn_setup():
        import jax, jax.numpy as jnp
        import numpy as np

        def _rope_tables(T, d):
            half = d // 2
            i = jnp.arange(half, dtype=jnp.float32)
            theta = 10000.0 ** (-2.0 * i / d)
            m = jnp.arange(T, dtype=jnp.float32)[:, None]
            ang = m * theta[None, :]
            return (jnp.cos(ang), jnp.sin(ang))

        def _rotate(v, cos, sin):
            B, T, d = v.shape
            half = d // 2
            v2 = v.reshape(B, T, half, 2)
            even, odd = (v2[..., 0], v2[..., 1])
            c = cos[None, :, :]
            s = sin[None, :, :]
            new_even = even * c - odd * s
            new_odd = even * s + odd * c
            return jnp.stack([new_even, new_odd], axis=-1).reshape(B, T, d)
        key = jax.random.key(seed)
        k1, k2, k3, k4 = jax.random.split(key, 4)
        B, T, d = (4, 256, 128)
        x = jax.random.normal(k1, (B, T, d), dtype=jnp.float32)
        scale = 0.02
        Wq = jax.random.normal(k2, (d, d), dtype=jnp.float32) * scale
        Wk = jax.random.normal(k3, (d, d), dtype=jnp.float32) * scale
        Wv = jax.random.normal(k4, (d, d), dtype=jnp.float32) * scale
        return {'x': x, 'Wq': Wq, 'Wk': Wk, 'Wv': Wv}
    _L0_attn_in = _L0_attn_setup()

    def _L0_ffn_setup():
        import jax, jax.numpy as jnp
        import numpy as np
        DIM = 128
        DEPTH = 2
        HEADS = 8
        DIM_HEAD = 64
        WINDOW = 64
        INNER = HEADS * DIM_HEAD
        HID = int(DIM * 4 * 2 / 3)
        B, N = (2, 1024)
        QK_SCALE = 8.0

        def shift_token(t):
            t1, t2 = jnp.split(t, 2, axis=-1)
            t2 = jnp.pad(t2, ((0, 0), (1, 0), (0, 0)))[:, :-1]
            return jnp.concatenate([t1, t2], axis=-1)

        def l2norm(t):
            return t / jnp.clip(jnp.linalg.norm(t, axis=-1, keepdims=True), 1e-12)

        def rotate_half(x):
            x1, x2 = jnp.split(x, 2, axis=-1)
            return jnp.concatenate([-x2, x1], axis=-1)

        def rotary_xpos(q, k):
            n = q.shape[-2]
            half_idx = jnp.arange(0, DIM_HEAD, 2, dtype=jnp.float32)
            inv_freq = 1.0 / 10000.0 ** (half_idx / DIM_HEAD)
            t = jnp.arange(n, dtype=jnp.float32)
            freqs = t[:, None] * inv_freq[None, :]
            freqs = jnp.concatenate([freqs, freqs], axis=-1)
            base = (half_idx + 0.4 * DIM_HEAD) / (1.4 * DIM_HEAD)
            power = (t - n // 2) / float(WINDOW // 2)
            scale = base[None, :] ** power[:, None]
            scale = jnp.concatenate([scale, scale], axis=-1)
            cos, sin = (jnp.cos(freqs), jnp.sin(freqs))
            q = q * cos * scale + rotate_half(q) * sin * scale
            k = k * cos / scale + rotate_half(k) * sin / scale
            return (q, k)

        def local_attention(q, k, v):
            b, h, n, d = q.shape
            w = n // WINDOW
            bq = q.reshape(b, h, w, WINDOW, d) * QK_SCALE
            bk = k.reshape(b, h, w, WINDOW, d)
            bv = v.reshape(b, h, w, WINDOW, d)

            def look_around(t):
                p = jnp.pad(t, ((0, 0), (0, 0), (1, 0), (0, 0), (0, 0)))
                return jnp.concatenate([p[:, :, :w], p[:, :, 1:]], axis=3)
            bk, bv = (look_around(bk), look_around(bv))
            bt = jnp.arange(n).reshape(w, WINDOW)
            btp = jnp.pad(bt, ((1, 0), (0, 0)), constant_values=-1)
            btk = jnp.concatenate([btp[:w], btp[1:]], axis=1)
            sim = jnp.einsum('bhwid,bhwjd->bhwij', bq, bk)
            i = bt[:, :, None]
            j = btk[:, None, :]
            mask = (i < j) | (i > j + WINDOW) | (j == -1)
            sim = jnp.where(mask, -jnp.finfo(sim.dtype).max, sim)
            attn = jax.nn.softmax(sim, axis=-1)
            out = jnp.einsum('bhwij,bhwjd->bhwid', attn, bv)
            return out.reshape(b, h, n, d)

        def _layer(x, wqkv, qs, ksc, wo, lg, lb, w1, b1, w2, b2):
            b, n, _ = x.shape
            h = shift_token(x)
            qkv = h @ wqkv
            q, k, v = jnp.split(qkv, 3, axis=-1)
            to_heads = lambda t: t.reshape(b, n, HEADS, DIM_HEAD).transpose(0, 2, 1, 3)
            q, k, v = (to_heads(q), to_heads(k), to_heads(v))
            q = l2norm(q) * qs
            k = l2norm(k) * ksc
            q, k = rotary_xpos(q, k)
            o = local_attention(q, k, v)
            o = o.transpose(0, 2, 1, 3).reshape(b, n, INNER)
            x = x + o @ wo
            h = shift_token(x)
            mu = h.mean(-1, keepdims=True)
            var = h.var(-1, keepdims=True)
            h = (h - mu) / jnp.sqrt(var + 1e-05) * lg + lb
            h = h @ w1 + b1
            a, g = jnp.split(h, 2, axis=-1)
            h = a * jax.nn.gelu(g, approximate=False)
            x = x + h @ w2 + b2
            return x
        key = jax.random.key(seed)
        ks = jax.random.split(key, 6)
        return {'x': jax.random.normal(ks[0], (B, N, DIM), jnp.float32), 'wqkv': jax.random.normal(ks[1], (DEPTH, DIM, 3 * INNER), jnp.float32) * 0.02, 'q_scale': jnp.ones((DEPTH, DIM_HEAD), jnp.float32), 'k_scale': jnp.ones((DEPTH, DIM_HEAD), jnp.float32), 'wo': jax.random.normal(ks[2], (DEPTH, INNER, DIM), jnp.float32) * 0.02, 'ln_g': jnp.ones((DEPTH, DIM), jnp.float32), 'ln_b': jnp.zeros((DEPTH, DIM), jnp.float32), 'w1': jax.random.normal(ks[3], (DEPTH, DIM, 2 * HID), jnp.float32) * 0.02, 'b1': jnp.zeros((DEPTH, 2 * HID), jnp.float32), 'w2': jax.random.normal(ks[4], (DEPTH, HID, DIM), jnp.float32) * 0.02, 'b2': jnp.zeros((DEPTH, DIM), jnp.float32)}
    _L0_ffn_in = _L0_ffn_setup()
    _d = {'L0_attn_x': _L0_attn_in['x'], 'L0_attn_Wq': _L0_attn_in['Wq'], 'L0_attn_Wk': _L0_attn_in['Wk'], 'L0_attn_Wv': _L0_attn_in['Wv'], 'L0_ffn_wqkv': _L0_ffn_in['wqkv'], 'L0_ffn_q_scale': _L0_ffn_in['q_scale'], 'L0_ffn_k_scale': _L0_ffn_in['k_scale'], 'L0_ffn_wo': _L0_ffn_in['wo'], 'L0_ffn_ln_g': _L0_ffn_in['ln_g'], 'L0_ffn_ln_b': _L0_ffn_in['ln_b'], 'L0_ffn_w1': _L0_ffn_in['w1'], 'L0_ffn_b1': _L0_ffn_in['b1'], 'L0_ffn_w2': _L0_ffn_in['w2'], 'L0_ffn_b2': _L0_ffn_in['b2']}
    _x0 = _d['L0_attn_x']
    _d['L0_attn_x'] = jax.random.normal(jax.random.fold_in(jax.random.key(seed), 1), (1, 2048, 128), dtype=_x0.dtype)
    del _x0
    return _d

def reference(L0_attn_x, L0_attn_Wq, L0_attn_Wk, L0_attn_Wv, L0_ffn_wqkv, L0_ffn_q_scale, L0_ffn_k_scale, L0_ffn_wo, L0_ffn_ln_g, L0_ffn_ln_b, L0_ffn_w1, L0_ffn_b1, L0_ffn_w2, L0_ffn_b2):

    def _L0_attn_ref(x, Wq, Wk, Wv):
        import jax, jax.numpy as jnp
        import numpy as np

        def _rope_tables(T, d):
            half = d // 2
            i = jnp.arange(half, dtype=jnp.float32)
            theta = 10000.0 ** (-2.0 * i / d)
            m = jnp.arange(T, dtype=jnp.float32)[:, None]
            ang = m * theta[None, :]
            return (jnp.cos(ang), jnp.sin(ang))

        def _rotate(v, cos, sin):
            B, T, d = v.shape
            half = d // 2
            v2 = v.reshape(B, T, half, 2)
            even, odd = (v2[..., 0], v2[..., 1])
            c = cos[None, :, :]
            s = sin[None, :, :]
            new_even = even * c - odd * s
            new_odd = even * s + odd * c
            return jnp.stack([new_even, new_odd], axis=-1).reshape(B, T, d)
        B, T, d = x.shape
        cos, sin = _rope_tables(T, d)
        Q = jnp.einsum('btd,ed->bte', x, Wq)
        K = jnp.einsum('btd,ed->bte', x, Wk)
        V = jnp.einsum('btd,ed->bte', x, Wv)
        Qr = _rotate(Q, cos, sin)
        Kr = _rotate(K, cos, sin)
        scores = jnp.einsum('bqd,bkd->bqk', Qr, Kr) / jnp.sqrt(jnp.float32(d))
        mask = jnp.tril(jnp.ones((T, T), dtype=bool), k=1)
        scores = jnp.where(mask[None, :, :], scores, -jnp.inf)
        attn = jax.nn.softmax(scores, axis=-1)
        out = jnp.einsum('bqk,bkd->bqd', attn, V)
        return out

    def _L0_ffn_ref(x, wqkv, q_scale, k_scale, wo, ln_g, ln_b, w1, b1, w2, b2):
        import jax, jax.numpy as jnp
        import numpy as np
        DIM = 128
        DEPTH = 2
        HEADS = 8
        DIM_HEAD = 64
        WINDOW = 64
        INNER = HEADS * DIM_HEAD
        HID = int(DIM * 4 * 2 / 3)
        B, N = (2, 1024)
        QK_SCALE = 8.0

        def shift_token(t):
            t1, t2 = jnp.split(t, 2, axis=-1)
            t2 = jnp.pad(t2, ((0, 0), (1, 0), (0, 0)))[:, :-1]
            return jnp.concatenate([t1, t2], axis=-1)

        def l2norm(t):
            return t / jnp.clip(jnp.linalg.norm(t, axis=-1, keepdims=True), 1e-12)

        def rotate_half(x):
            x1, x2 = jnp.split(x, 2, axis=-1)
            return jnp.concatenate([-x2, x1], axis=-1)

        def rotary_xpos(q, k):
            n = q.shape[-2]
            half_idx = jnp.arange(0, DIM_HEAD, 2, dtype=jnp.float32)
            inv_freq = 1.0 / 10000.0 ** (half_idx / DIM_HEAD)
            t = jnp.arange(n, dtype=jnp.float32)
            freqs = t[:, None] * inv_freq[None, :]
            freqs = jnp.concatenate([freqs, freqs], axis=-1)
            base = (half_idx + 0.4 * DIM_HEAD) / (1.4 * DIM_HEAD)
            power = (t - n // 2) / float(WINDOW // 2)
            scale = base[None, :] ** power[:, None]
            scale = jnp.concatenate([scale, scale], axis=-1)
            cos, sin = (jnp.cos(freqs), jnp.sin(freqs))
            q = q * cos * scale + rotate_half(q) * sin * scale
            k = k * cos / scale + rotate_half(k) * sin / scale
            return (q, k)

        def local_attention(q, k, v):
            b, h, n, d = q.shape
            w = n // WINDOW
            bq = q.reshape(b, h, w, WINDOW, d) * QK_SCALE
            bk = k.reshape(b, h, w, WINDOW, d)
            bv = v.reshape(b, h, w, WINDOW, d)

            def look_around(t):
                p = jnp.pad(t, ((0, 0), (0, 0), (1, 0), (0, 0), (0, 0)))
                return jnp.concatenate([p[:, :, :w], p[:, :, 1:]], axis=3)
            bk, bv = (look_around(bk), look_around(bv))
            bt = jnp.arange(n).reshape(w, WINDOW)
            btp = jnp.pad(bt, ((1, 0), (0, 0)), constant_values=-1)
            btk = jnp.concatenate([btp[:w], btp[1:]], axis=1)
            sim = jnp.einsum('bhwid,bhwjd->bhwij', bq, bk)
            i = bt[:, :, None]
            j = btk[:, None, :]
            mask = (i < j) | (i > j + WINDOW) | (j == -1)
            sim = jnp.where(mask, -jnp.finfo(sim.dtype).max, sim)
            attn = jax.nn.softmax(sim, axis=-1)
            out = jnp.einsum('bhwij,bhwjd->bhwid', attn, bv)
            return out.reshape(b, h, n, d)

        def _layer(x, wqkv, qs, ksc, wo, lg, lb, w1, b1, w2, b2):
            b, n, _ = x.shape
            h = shift_token(x)
            qkv = h @ wqkv
            q, k, v = jnp.split(qkv, 3, axis=-1)
            to_heads = lambda t: t.reshape(b, n, HEADS, DIM_HEAD).transpose(0, 2, 1, 3)
            q, k, v = (to_heads(q), to_heads(k), to_heads(v))
            q = l2norm(q) * qs
            k = l2norm(k) * ksc
            q, k = rotary_xpos(q, k)
            o = local_attention(q, k, v)
            o = o.transpose(0, 2, 1, 3).reshape(b, n, INNER)
            x = x + o @ wo
            h = shift_token(x)
            mu = h.mean(-1, keepdims=True)
            var = h.var(-1, keepdims=True)
            h = (h - mu) / jnp.sqrt(var + 1e-05) * lg + lb
            h = h @ w1 + b1
            a, g = jnp.split(h, 2, axis=-1)
            h = a * jax.nn.gelu(g, approximate=False)
            x = x + h @ w2 + b2
            return x
        for l in range(DEPTH):
            x = _layer(x, wqkv[l], q_scale[l], k_scale[l], wo[l], ln_g[l], ln_b[l], w1[l], b1[l], w2[l], b2[l])
        return x
    x = L0_attn_x
    x = _layernorm(x + _L0_attn_ref(x, L0_attn_Wq, L0_attn_Wk, L0_attn_Wv), axis=-1)
    x = _layernorm(x + _L0_ffn_ref(x, L0_ffn_wqkv, L0_ffn_q_scale, L0_ffn_k_scale, L0_ffn_wo, L0_ffn_ln_g, L0_ffn_ln_b, L0_ffn_w1, L0_ffn_b1, L0_ffn_w2, L0_ffn_b2), axis=-1)
    return x

_drawn_inputs = setup_inputs


def setup_inputs(seed=0):
    import zlib

    import numpy as np

    out = dict(_drawn_inputs(seed))
    spreads = {'L0_ffn_q_scale': (1.0, 0.6),
     'L0_ffn_k_scale': (1.0, 0.6),
     'L0_ffn_ln_g': (1.0, 0.6),
     'L0_ffn_ln_b': (0.0, 0.8),
     'L0_ffn_b1': (0.0, 0.8),
     'L0_ffn_b2': (0.0, 0.401)}
    factors = {'L0_attn_Wq': 8.0,
     'L0_attn_Wk': 8.0,
     'L0_attn_Wv': 4.271,
     'L0_ffn_wqkv': 4.145,
     'L0_ffn_wo': 4.121,
     'L0_ffn_w1': 6.219,
     'L0_ffn_w2': 6.123}
    for name, (base, spread) in spreads.items():
        noise = np.random.default_rng([zlib.crc32(name.encode()), seed]).standard_normal(out[name].shape)
        drawn = base * np.exp(spread * noise) if base else spread * noise
        out[name] = jnp.asarray(drawn.astype(out[name].dtype))
    for name, factor in factors.items():
        out[name] = (out[name] * factor).astype(out[name].dtype)
    return out
```

```python
import concourse.bass as bass
from concourse import mybir
from contextlib import ExitStack
import numpy as np

P = 128
N = 2048
TILES = N // P
D = 128
DEPTH = 2
HEADS = 8
DH = 64
PAIRS = HEADS // 2
WINDOW = 64
INNER = HEADS * DH
HID = int(D * 4 * 2 / 3)
CHUNKS = [(c, min(P, HID - c)) for c in range(0, HID, P)]
GROUP = 512
GROUPS = N // GROUP
NEG = -3.0e38
EPS = 1e-5
HALVES = ((0, 64), (64, 128))


def build(nc, x, w_qkv1, rope1, w_qkv, q_scale, k_scale, w_o, ln_g, ln_b, w_1, b_1, w_2, b_2, xpos, out):
    F = mybir.dt.float32
    BF = mybir.dt.bfloat16
    ALU = mybir.AluOpType
    ACT = mybir.ActivationFunctionType
    AX = mybir.AxisListType
    ctx = ExitStack()
    with ctx:
        def sb(name, shape, dt=F):
            return ctx.enter_context(nc.sbuf_tensor(name, shape, dt))

        def sem(name):
            return ctx.enter_context(nc.semaphore(name))

        ident = sb("ident", [P, P])
        ident_bf = sb("ident_bf", [P, P], BF)
        centre = sb("centre", [P, P])
        average = sb("average", [P, P])
        mask1 = sb("mask1", [P, P + 1], BF)
        mask2 = sb("mask2", [P, 2, 2, 2, WINDOW], BF)
        mask2_first = sb("mask2_first", [P, 2, 2, 2, WINDOW], BF)
        wqkv = sb("wqkv", [P, DEPTH, 3 * INNER])
        wo = sb("wo", [P, DEPTH, PAIRS, D])
        w1 = sb("w1", [P, DEPTH, 2 * HID])
        w2 = sb("w2", [P, DEPTH, len(CHUNKS), D])
        b1 = sb("b1", [P, DEPTH, 2, len(CHUNKS)])
        cols = sb("cols", [P, DEPTH, 3])
        table = sb("table", [P, 4, TILES, DH])
        qkscale = sb("qkscale", [P, DEPTH, 2, DH])
        scaled = sb("scaled", [P, 2, 2, TILES, DH])
        x0 = sb("x0", [P, N + 1])
        xa = sb("xa", [P, N + 1])
        xb = sb("xb", [P, N + 1])
        flat = scaled[:].rearrange("p a s t d -> p (a s t d)")
        x_tok = flat[:, 0:N].rearrange("p (t d) -> p t d", d=D)
        w1st = flat[:, N:N + 5 * P].rearrange("p (a e) -> p a e", a=5)
        qk_all = sb("qk_all", [P, TILES, 2 * HEADS, DH])
        arena = qk_all[:].rearrange("p t h d -> p (t h d)")
        rope = arena[:, 0:2 * N].rearrange("p (a n) -> p a n", a=2)
        xt, qt, kt = (arena[:, N * a:N * (a + 1)] for a in (2, 3, 4))
        v1 = arena[:, 5 * N:6 * N].rearrange("p (t d) -> p t d", d=D)
        vx = arena[0:1, 6 * N:7 * N].rearrange("p (t d) -> p t d", d=D)
        rope_tmp = arena[:, 7 * N:7 * N + 2 * GROUP].rearrange("p (a n) -> p a n", a=2)
        stats = sb("stats", [P, TILES, 6])
        mean_var = sb("mean_var", [P, TILES, 2])
        std = sb("std", [P, TILES])
        rstd = sb("rstd", [P, TILES])
        nmax = sb("nmax", [P, 2])
        bias = sb("bias", [P, 2])
        rsum = sb("rsum", [P, 2])
        rinv = sb("rinv", [P, 2])
        hs = sb("hs", [P, 2, P])
        v_tmp = sb("v_tmp", [P, 2, INNER])
        v_dram = nc.dram_tensor("v_dram", (TILES, P, INNER), F, kind="Internal").ap()
        ss = sb("ss", [P, TILES, 2 * HEADS])
        ssm = sb("ssm", [P, TILES, 2 * HEADS])
        rn = sb("rn", [P, TILES, 2 * HEADS])
        big = sb("big", [P, 7 * 1024])
        pbuf = big[:, 0:2 * N].rearrange("p (u n) -> p u n", u=2)
        ptb = big[:, 2 * N:2 * N + 1024].rearrange("p (b n) -> p b n", b=2)
        ptx = big[:, 2 * N + 1024:2 * N + 1152]
        sq = big[:, 0:2048].rearrange("p (u n) -> p u n", u=2)
        qn, ts, tc = (big[:, 1024 * a:1024 * (a + 1)].rearrange("p (h d) -> p h d", d=DH) for a in (0, 1, 2))
        qr, sc, pt2 = (big[:, 1024 * a:1024 * (a + 1)] for a in (2, 3, 4))
        pr = big[:, 5 * 1024:7 * 1024].rearrange("p (u n) -> p u n", u=2)
        qbd = sb("qbd", [P, PAIRS, 2, 2, WINDOW])
        kring = sb("kring", [P, PAIRS, 4, WINDOW])
        vs = sb("vs", [P, 2, INNER])
        vm = sb("vm", [P, 2, INNER])
        ot = sb("ot", [P, PAIRS, P])
        smax = sb("smax", [P, 8])
        ssum = sb("ssum", [P, 8])
        sinv = sb("sinv", [P, 8])
        eps = sb("eps", [P, 1])
        hc = qk_all[:, 0:2, :, :].rearrange("p t h d -> p (t h d)")
        rs = qk_all[:, 2:4, :, :].rearrange("p t h d -> p (t h d)")
        hn = qk_all[:, 4:6, :, :].rearrange("p t h d -> p (t h d)")
        sqf = qk_all[:, 6:8, :, :].rearrange("p t h d -> p (t h d)")
        ge = qk_all[:, 8:10, :, :].rearrange("p t h d -> p (t h d)")
        gu = qk_all[:, 10:12, :, :].rearrange("p t h d -> p (t h d)")
        fin = qk_all[:, 12:14, :, :].rearrange("p t h d -> p (t h d)")
        y_out = qk_all[:, 14:16, :, :].rearrange("p t h d -> p (t h d)").rearrange("p (t d) -> p t d", d=D)

        ps = ctx.enter_context(nc.psum_tensor("ps", [P, 8, 512], F))

        s_x, s_w1st, s_rope, s_wqkv, s_wrest, s_tab = [sem(n) for n in (
            "x_loaded", "w1st_loaded", "rope_loaded", "wqkv_loaded", "wrest_loaded", "tables_loaded")]
        s_const, s_cchain, s_scaled = sem("constants_made"), sem("constants_step"), sem("tables_scaled")
        s_xtp, s_xt = sem("xt_in_psum"), sem("xt_saved")
        s_qkp, s_rc, s_rsn, s_qkt = sem("qk_in_psum"), sem("rope_cos"), sem("rope_sin"), sem("qk_roped")
        s_vp, s_v = sem("v1_in_psum"), sem("v1_saved")
        s_vx = sem("v1_rows_moved")
        s_s1, s_m1, s_b1, s_e1 = sem("scores1"), sem("max1"), sem("bias1"), sem("exp1")
        s_t1, s_te1, s_pv1, s_ri1, s_o1 = sem("p1_transposed"), sem("pt1_saved"), sem("out1"), sem("rinv1"), sem("res1")
        s_bs, s_ba, s_sd, s_rd, s_ln1 = sem("bn_stats"), sem("bn_aggr"), sem("std_made"), sem("rstd_made"), sem("normed")
        s_ve, s_eps = sem("var_eps"), sem("eps_made")
        s_x0p, s_x0, s_xac = sem("x0_in_psum"), sem("x0_saved"), sem("xa_copied")
        s_hs, s_proj, s_sq, s_qs, s_vsv, s_ks, s_ss = [sem(n) for n in (
            "hs_staged", "qkv_in_psum", "squared", "q_saved", "v_saved", "k_saved", "sumsq_made")]
        s_nm, s_nq, s_nr = sem("norm_clipped"), sem("norm_rooted"), sem("norm_inverted")
        s_qn, s_tc, s_ts, s_qr = sem("qk_normed"), sem("times_cos"), sem("times_sin"), sem("qk_rotated")
        s_tt, s_kev, s_qev = sem("qk_transposed"), sem("kt_saved"), sem("qt_saved")
        s_s, s_mx, s_sub, s_exp, s_sum, s_inv, s_pn = [sem(n) for n in (
            "scores", "score_max", "score_shifted", "score_exp", "exp_sum", "exp_inv", "probs")]
        s_pt, s_pte, s_pv, s_oe, s_y, s_xb = [sem(n) for n in (
            "probs_transposed", "pt_saved", "pv_in_psum", "ot_saved", "attn_y", "xb_made")]
        s_vout = [sem("v_written_0"), sem("v_written_1")]
        s_vst = [sem("v_staged_0"), sem("v_staged_1")]
        s_cp, s_hc, s_sqf, s_vp2, s_ln, s_rs, s_hr, s_hn = [sem(n) for n in (
            "centred_in_psum", "centred_saved", "centred_squared", "var_in_psum", "var_log", "rstd_row", "hn_scaled", "hn_made")]
        s_g, s_a, s_ge, s_gu, s_y2, s_xf = [sem(n) for n in (
            "gate_in_psum", "value_in_psum", "gelu_made", "gated", "ffn_y", "ffn_out")]
        s_fs, s_ft, s_fo, s_out = sem("final_sum"), sem("final_in_psum"), sem("final_normed"), sem("out_written")

        def after(eng, semaphore, value):
            if not isinstance(value, int) or value > 0:
                eng.wait_ge(semaphore, value)

        def tiles_in_pairs(eng, first, loop_from, loop_to, last, step):
            for t in range(first, loop_from):
                step(t, t % 2)
            with eng.Fori(loop_from // 2, loop_to // 2) as pair:
                for u in range(2):
                    step(2 * pair + u, u)
            for t in range(loop_to, last):
                step(t, t % 2)

        def staged(l, t, u):
            layer = 16 * (3 * TILES // 2 - (1 - u))
            return layer * l + 24 * (t - u) + (48 if u else 32)

        def keys1(i):
            return min(P * (i + 1) + 1, N)

        ends1 = list(np.cumsum([len(range(0, i + 1, 4)) + (keys1(i) > P * (i + 1)) for i in range(TILES)]).tolist())

        SCALE1 = 1.0 / float(np.sqrt(np.float32(D)))
        block = ctx.enter_context(nc.Block())

        @block.sync
        def _(sp):
            sp.dma_start(x_tok[:], x.rearrange("b (t p) d -> p (b t) d", p=P)).then_inc(s_x, 16)
            sp.dma_start(w1st[:], w_qkv1.rearrange("a p e -> p a e")).then_inc(s_w1st, 16)
            for c in range(2):
                sp.dma_start(rope[:, c, :], rope1[c]).then_inc(s_rope, 16)
            sp.dma_start(wqkv[:], w_qkv.rearrange("l p n -> p l n")).then_inc(s_wqkv, 16)
            for s in range(4):
                sp.dma_start(table[:, s, :, :], xpos[s].rearrange("(t p) d -> p t d", p=P)).then_inc(s_tab, 16)
            for s, v in enumerate((q_scale, k_scale)):
                for l in range(DEPTH):
                    sp.dma_start(qkscale[:, l, s, :], v[l:l + 1, :].to_broadcast([P, DH])).then_inc(s_tab, 16)
            for l in range(DEPTH):
                sp.dma_start(wo[:, l], w_o[l].rearrange("(g p) n -> p g n", p=P)).then_inc(s_wrest, 16)
                sp.dma_start(w1[:, l], w_1[l]).then_inc(s_wrest, 16)
                for j, (c, m) in enumerate(CHUNKS):
                    sp.dma_start(w2[0:m, l, j, :], w_2[l, c:c + m, :]).then_inc(s_wrest, 16)
                    for ag in range(2):
                        sp.dma_start(b1[0:m, l, ag, j:j + 1],
                                     b_1[l, ag * HID + c:ag * HID + c + m].rearrange("(p o) -> p o", o=1)).then_inc(s_wrest, 16)
                for j, v in enumerate((ln_g, ln_b, b_2)):
                    sp.dma_start(cols[:, l, j:j + 1], v[l].rearrange("(p o) -> p o", o=1)).then_inc(s_wrest, 16)
            sp.wait_ge(s_v, 4)
            sp.dma_start(vx[0:1, :, :], v1[0:1, :, :]).then_inc(s_vx, 16)
            for l in range(DEPTH):
                def write_v(t, u):
                    sp.wait_ge(s_vsv, TILES * l + t + 1)
                    sp.dma_start(v_dram[bass.ds(t, 1)].rearrange("o p n -> p (o n)"), v_tmp[:, u, :]).then_inc(s_vout[u], 16)
                tiles_in_pairs(sp, 0, 2, TILES, TILES, write_v)
                for u in range(2):
                    sp.wait_ge(s_vout[u], 8 * TILES * (l + 1))

                def stage(t, u):
                    T = TILES * l + t
                    after(sp, s_pv, T - 1)
                    sp.dma_start(vs[:, u, :], v_dram[bass.ds(t, 1)].rearrange("o p n -> p (o n)")).then_inc(s_vst[u], 16)
                    sp.dma_start(vm[0:64, u, :], v_dram[bass.ds(t, 1), 0:64].rearrange("o p n -> p (o n)")).then_inc(s_vst[u], 16)
                    if not (isinstance(t, int) and t == 0):
                        sp.dma_start(vm[64:128, u, :], v_dram[bass.ds(t - 1, 1), 64:128].rearrange("o p n -> p (o n)")).then_inc(s_vst[u], 16)
                tiles_in_pairs(sp, 0, 2, TILES, TILES, stage)
            for j in range(GROUPS):
                sp.wait_ge(s_fo, 4 * (j + 1))
                sp.dma_start(out.rearrange("b (t p) d -> p (b t) d", p=P)[:, 4 * j:4 * j + 4, :],
                             y_out[:, 4 * j:4 * j + 4, :]).then_inc(s_out, 16)
            sp.wait_ge(s_out, 16 * GROUPS)

        @block.gpsimd
        def _(pool):
            g = nc.gpsimd
            steps = [0]

            def chain(ins):
                steps[0] += 1
                ins.then_inc(s_cchain, 1)
                pool.wait_ge(s_cchain, steps[0])

            chain(g.memset(ident[:], 0.0))
            chain(g.affine_select(out=ident[:], in_=ident[:], compare_op=ALU.not_equal, fill=1.0, base=0,
                                  pattern=[[-1, P]], channel_multiplier=1))
            chain(g.tensor_copy(ident_bf[:], ident[:]))
            chain(g.memset(mask1[:], 0.0))
            chain(g.affine_select(out=mask1[:], in_=mask1[:], compare_op=ALU.is_ge, fill=NEG, base=1,
                                  pattern=[[-1, P + 1]], channel_multiplier=1))
            chain(g.memset(average[:], 1.0 / D))
            chain(g.tensor_scalar(centre[:], ident[:], -1.0 / D, None, ALU.add))
            for m in (mask2, mask2_first):
                chain(g.memset(m[:], 0.0))
                for a, b in HALVES:
                    for w in range(2):
                        for half in range(2):
                            own = half == w
                            v = m[a:b, :, w, half, :]
                            chain(g.affine_select(out=v, in_=v, compare_op=ALU.is_ge, fill=NEG, base=0,
                                                  pattern=[[0, 2], [-1 if own else 1, WINDOW]],
                                                  channel_multiplier=1 if own else -1))
            chain(g.memset(mask2_first[:, :, 0, 1, :], NEG))
            for buffer in (qbd, kring, vm):
                chain(g.memset(buffer[:], 0.0))
            for buffer in (x0, xa, xb):
                chain(g.memset(buffer[64:128, 0:1], 0.0))
            g.memset(x0[0:64, N:N + 1], 0.0).then_inc(s_const, 1)

            for l in range(DEPTH):
                if l == 0:
                    pool.wait_ge(s_tab, 16 * 8)
                src = xa if l else x0
                if l:
                    pool.wait_ge(s_xf, 2 * GROUPS * l)
                else:
                    pool.wait_ge(s_x0, 2 * GROUPS)

                def stage_h(t, u):
                    T = TILES * l + t
                    after(pool, s_proj, 3 * (T - 1))
                    g.tensor_copy(hs[:, u, :], src[:, bass.ds(P * t, P)]).then_inc(s_hs, 1)
                    row = bass.ds(t, 1)
                    g.tensor_tensor(scaled[:, 0, :, row, :].rearrange("p s o d -> p s (o d)"),
                                    table[:, 0:3:2, row, :].rearrange("p s o d -> p s (o d)"),
                                    qkscale[:, l], ALU.mult).then_inc(s_scaled, 1)
                    for h in range(2):
                        o, i = slice(32 * h, 32 * h + 32), slice(32 * (1 - h), 32 * (1 - h) + 32)
                        g.tensor_tensor(scaled[:, 1, :, row, o].rearrange("p s o d -> p s (o d)"),
                                        table[:, 1:4:2, row, o].rearrange("p s o d -> p s (o d)"),
                                        qkscale[:, l, :, i], ALU.mult).then_inc(s_scaled, 1)
                tiles_in_pairs(pool, 0, 2, TILES, TILES, stage_h)

                pool.wait_ge(s_scaled, 3 * TILES * (l + 1))

                def front(t, T):
                    pool.wait_ge(s_qn, T + 1)
                    after(pool, s_tt, 2 * T)
                    g.tensor_tensor(tc.rearrange("p (s h) d -> p s h d", s=2), qn.rearrange("p (s h) d -> p s h d", s=2),
                                    scaled[:, 0, :, bass.ds(t, 1), :].to_broadcast([P, 2, HEADS, DH]),
                                    ALU.mult).then_inc(s_tc, 1)

                def step(t, u):
                    T = TILES * l + t
                    if not (isinstance(t, int) and t + 1 >= TILES):
                        front(t + 1, T + 1)
                    if not (isinstance(t, int) and t < 0):
                        pool.wait_ge(s_inv, T + 1)
                        after(pool, s_pt, 2 * (T - 1))
                        g.tensor_tensor(pr[:, u, :].rearrange("p (b k) -> p b k", b=8), sc.rearrange("p (b k) -> p b k", b=8),
                                        sinv[:, :, None].to_broadcast([P, 8, P]), ALU.mult).then_inc(s_pn, 1)
                tiles_in_pairs(pool, -1, 2, TILES - 2, TILES, step)

        @block.tensor
        def _(pe):
            mm, tr = nc.tensor.matmul, nc.tensor.transpose
            pe.wait_ge(s_const, 1)
            pe.wait_ge(s_x, 16)
            for t in range(TILES):
                ins = tr(ps[:, t // 4, P * (t % 4):P * (t % 4 + 1)], x_tok[:, t, :], ident[:])
                if t % 4 == 3:
                    ins.then_inc(s_xtp, 1)
            pe.wait_ge(s_w1st, 16)
            for j in range(GROUPS):
                pe.wait_ge(s_xt, j + 1)
                for s in range(2):
                    n = 2 * j + s
                    after(pe, s_rsn, n - 1)
                    for r in range(2):
                        ins = mm(ps[:, 4 + 2 * (n % 2) + r, :], w1st[:, 2 * s + r, :], xt[:, GROUP * j:GROUP * (j + 1)],
                                 start=True, stop=True)
                    ins.then_inc(s_qkp, 1)
            for t in range(TILES):
                ins = mm(ps[:, t // 4, P * (t % 4):P * (t % 4 + 1)], xt[:, P * t:P * (t + 1)], w1st[:, 4, :], start=True, stop=True)
                if t % 4 == 3:
                    ins.then_inc(s_vp, 1)
            lots = 0

            def scores1(i):
                if i == 0:
                    pe.wait_ge(s_v, 4)
                    pe.wait_ge(s_qkt, 2 * GROUPS)
                else:
                    pe.wait_ge(s_e1, i)
                n = keys1(i)
                d, e = P * i, min(P * (i + 1), n)
                masked = (d // 512, (n - 1) // 512)
                for c in range(0, n, 512):
                    m = min(512, n - c)
                    mm(ps[:, c // 512, 0:m], qt[:, P * i:P * (i + 1)], kt[:, c:c + m], start=True,
                       stop=c // 512 not in masked, skip_group_check=True)
                ins = mm(ps[:, d // 512, d % 512:d % 512 + P], ident_bf[:], mask1[:, 0:P], start=False, stop=True, skip_group_check=True)
                if n > e:
                    ins = mm(ps[:, e // 512, e % 512:e % 512 + 1], ident_bf[:], mask1[:, P:P + 1], start=False, stop=True, skip_group_check=True)
                ins.then_inc(s_s1, 1)

            def output1(i):
                nonlocal lots
                pe.wait_ge(s_e1, i + 1)
                first = True
                groups = [list(range(k, min(k + 4, i + 1))) for k in range(0, i + 1, 4)]
                extra = keys1(i) > P * (i + 1)
                if extra:
                    groups.append(None)

                def transpose(group):
                    nonlocal lots
                    after(pe, s_te1, lots - 1)
                    bank = 4 + lots % 2
                    if group is None:
                        ins = tr(ps[0:1, bank, 0:P], pbuf[:, i % 2, P * (i + 1):P * (i + 1) + 1], ident[:])
                    else:
                        for a, k in enumerate(group):
                            ins = tr(ps[:, bank, P * a:P * (a + 1)], pbuf[:, i % 2, P * k:P * (k + 1)], ident[:])
                    ins.then_inc(s_t1, 1)
                    lots += 1
                    return lots - 1

                def product(group, lot, start, stop):
                    pe.wait_ge(s_te1, lot + 1)
                    if group is None:
                        pe.wait_ge(s_vx, 16)
                        ins = mm(ps[:, 6 + i % 2, 0:P], ptx[0:1, :], vx[0:1, i + 1, :], start=False, stop=True)
                    else:
                        for a, k in enumerate(group):
                            ins = mm(ps[:, 6 + i % 2, 0:P], ptb[:, lot % 2, P * a:P * (a + 1)], v1[:, k, :],
                                     start=start and a == 0, stop=stop and a == len(group) - 1)
                    return ins
                after(pe, s_o1, i - 1)
                lot = transpose(groups[0])
                for n, group in enumerate(groups):
                    after_this = transpose(groups[n + 1]) if n + 1 < len(groups) else None
                    ins = product(group, lot, n == 0, n == len(groups) - 1)
                    ins.then_inc(s_pv1, 1)
                    lot = after_this
            for i in range(TILES + 1):
                if i < TILES:
                    scores1(i)
                if i:
                    output1(i - 1)
            for t in range(TILES):
                pe.wait_ge(s_ln1, t + 1)
                ins = tr(ps[:, t // 4, P * (t % 4):P * (t % 4 + 1)], x_tok[:, t, :], ident[:])
                if t % 4 == 3:
                    ins.then_inc(s_x0p, 1)

            for l in range(DEPTH):
                pe.wait_ge(s_wqkv, 16)
                if l == 0:
                    pe.wait_ge(s_x0, 2 * GROUPS)

                def project(t, u):
                    T = TILES * l + t
                    pe.wait_ge(s_hs, T + 1)
                    after(pe, s_vsv, T - 1)
                    after(pe, s_ks, T - 1)
                    for a in range(3):
                        mm(ps[:, 3 * u + a, :], hs[:, u, :], wqkv[:, l, INNER * a:INNER * (a + 1)], start=True, stop=True).then_inc(s_proj, 1)
                tiles_in_pairs(pe, 0, 2, TILES, TILES, project)
                pe.wait_ge(s_vsv, TILES * (l + 1))
                pe.wait_ge(s_ks, TILES * (l + 1))
                pe.wait_ge(s_wrest, 16 * 28)

                def scores(t, T, u):
                    pe.wait_ge(s_qr, T + 1)
                    after(pe, s_qev, T)
                    for s, bank in ((1, 0), (0, 1)):
                        for g in range(PAIRS):
                            c = INNER * s + P * g
                            ins = tr(ps[:, bank, P * g:P * (g + 1)], qr[:, c:c + P], ident[:])
                        ins.then_inc(s_tt, 1)
                    after(pe, s_sub, T)
                    first = isinstance(t, int) and t == 0
                    for b in range(2):
                        mm(ps[:, 2 + b, :], ident_bf[:], (mask2_first if first else mask2)[:].rearrange("p g w a k -> p (g w a k)"),
                           start=True, stop=False, skip_group_check=True)
                    pe.wait_ge(s_kev, T + 1)
                    pe.wait_ge(s_qev, T + 1)
                    even = kring[:, :, 0:4:3, :] if u == 0 else kring[:, :, 1:3, :]
                    odd = kring[:, :, u:u + 3:2, :]
                    for g in range(PAIRS):
                        for w, keys in enumerate((even, odd)):
                            c = 256 * (g % 2) + P * w
                            ins = mm(ps[:, 2 + g // 2, c:c + P], qbd[:, g, w].rearrange("p h q -> p (h q)"), keys[:, g],
                                     start=False, stop=True, skip_group_check=True)
                    ins.then_inc(s_s, 1)

                def outputs(t, T, u):
                    pe.wait_ge(s_pn, T + 1)
                    after(pe, s_xb, 2 * T)
                    for b in range(2):
                        for a in range(4):
                            c = 512 * b + P * a
                            ins = tr(ps[:, 4 + b, P * a:P * (a + 1)], pr[:, u, c:c + P], ident[:])
                        ins.then_inc(s_pt, 1)
                    pe.wait_ge(s_vst[u], staged(l, t, u))
                    after(pe, s_oe, 2 * T)
                    for b in range(2):
                        pe.wait_ge(s_pte, 2 * T + b + 1)
                        for a in range(4):
                            g, w = 2 * b + a // 2, a % 2
                            c = 512 * b + P * a
                            ins = mm(ps[:, 6 + b, P * a:P * (a + 1)], (vs if w else vm)[:, u, P * g:P * (g + 1)], pt2[:, c:c + P],
                                     start=True, stop=True)
                    ins.then_inc(s_pv, 1)
                    pe.wait_ge(s_oe, 2 * T + 2)
                    for g in range(PAIRS):
                        ins = mm(ps[:, 4, 0:P], wo[:, l, g, :], ot[:, g, :], start=g == 0, stop=g == PAIRS - 1)
                    ins.then_inc(s_y, 1)

                def step(t, u):
                    T = TILES * l + t
                    if not (isinstance(t, int) and t >= TILES):
                        scores(t, T, u)
                    if not (isinstance(t, int) and t < 1):
                        outputs(t - 1, T - 1, 1 - u)
                tiles_in_pairs(pe, 0, 2, TILES, TILES + 1, step)

                for j in range(GROUPS + 1):
                    if j < GROUPS:
                        J = GROUPS * l + j
                        pe.wait_ge(s_xb, 2 * (TILES * l + 4 * j + 4))
                        if j >= 2:
                            pe.wait_ge(s_sqf, J - 1)
                            pe.wait_ge(s_hc, J - 1)
                        mm(ps[:, j % 2, :], centre[:], xb[:, GROUP * j:GROUP * (j + 1)], start=True, stop=True).then_inc(s_cp, 1)
                    if j:
                        J = GROUPS * l + j - 1
                        pe.wait_ge(s_sqf, J + 1)
                        mm(ps[:, 2 + j - 1, :], average[:], sqf[:, GROUP * (j - 1):GROUP * j], start=True, stop=True).then_inc(s_vp2, 1)

                pe.wait_ge(s_ln, l + 1)
                for j in range(GROUPS):
                    J = GROUPS * l + j
                    pe.wait_ge(s_hn, J + 1)
                    for c, (o, m) in enumerate(CHUNKS):
                        after(pe, s_gu, 3 * (J - 1) + c + 1)
                        mm(ps[0:m, 2 * c, :], w1[:, l, HID + o:HID + o + m], hn[:, GROUP * j:GROUP * (j + 1)],
                           start=True, stop=True).then_inc(s_g, 1)
                        mm(ps[0:m, 2 * c + 1, :], w1[:, l, o:o + m], hn[:, GROUP * j:GROUP * (j + 1)],
                           start=True, stop=True).then_inc(s_a, 1)
                    after(pe, s_xf, 2 * J)
                    for c, (o, m) in enumerate(CHUNKS):
                        pe.wait_ge(s_gu, 3 * J + c + 1)
                        ins = mm(ps[:, 6, :], w2[0:m, l, c, :], gu[0:m, GROUP * c:GROUP * (c + 1)],
                                 start=c == 0, stop=c == len(CHUNKS) - 1)
                    ins.then_inc(s_y2, 1)
            for t in range(TILES):
                pe.wait_ge(s_fs, 2 * (t // 4 + 1))
                ins = tr(ps[:, t // 4, P * (t % 4):P * (t % 4 + 1)], fin[:, P * t:P * (t + 1)], ident[:])
                if t % 4 == 3:
                    ins.then_inc(s_ft, 1)

        @block.scalar
        def _(act):
            act_fn = nc.scalar.activation
            for j in range(GROUPS):
                act.wait_ge(s_xtp, j + 1)
                act_fn(xt[:, GROUP * j:GROUP * (j + 1)], ps[:, j, :], ACT.Copy).then_inc(s_xt, 1)
            for j in range(GROUPS):
                act.wait_ge(s_vp, j + 1)
                act_fn(v1[:, 4 * j:4 * j + 4, :].rearrange("p t d -> p (t d)"), ps[:, j, :], ACT.Copy).then_inc(s_v, 1)
            lots = 0

            def save1(i):
                nonlocal lots
                groups = [min(4, i + 1 - k) for k in range(0, i + 1, 4)]
                if keys1(i) > P * (i + 1):
                    groups.append(0)
                for m in groups:
                    act.wait_ge(s_t1, lots + 1)
                    after(act, s_pv1, lots - 1)
                    if m:
                        act_fn(ptb[:, lots % 2, 0:P * m], ps[:, 4 + lots % 2, 0:P * m], ACT.Copy).then_inc(s_te1, 1)
                    else:
                        act_fn(ptx[0:1, :], ps[0:1, 4 + lots % 2, 0:P], ACT.Copy).then_inc(s_te1, 1)
                    lots += 1
            for i in range(TILES + 1):
                if i < TILES:
                    act.wait_ge(s_b1, i + 1)
                    if i >= 2:
                        act.wait_ge(s_t1, ends1[i - 2])
                        act.wait_ge(s_ri1, i - 1)
                    act_fn(pbuf[:, i % 2, 0:keys1(i)], ps[:, 0:4, :].rearrange("p b n -> p (b n)")[:, 0:keys1(i)], ACT.Exp,
                           bias=bias[:, i % 2:i % 2 + 1], scale=SCALE1, accum_out=rsum[:, i % 2:i % 2 + 1]).then_inc(s_e1, 1)
                if i:
                    save1(i - 1)
            act.wait_ge(s_ve, 1)
            act_fn(std[:], std[:], ACT.Sqrt).then_inc(s_sd, 1)
            for j in range(GROUPS):
                act.wait_ge(s_x0p, j + 1)
                act_fn(x0[0:64, GROUP * j:GROUP * (j + 1)], ps[0:64, j, :], ACT.Copy).then_inc(s_x0, 1)

            for l in range(DEPTH):
                def project(t, u):
                    T = TILES * l + t
                    qk = qk_all[:, bass.ds(t, 1), :, :].rearrange("p o h d -> p (o h d)")
                    act.wait_ge(s_proj, 3 * T + 1)
                    after(act, s_ss, T - 1)
                    act_fn(sq[:, u, 0:INNER], ps[:, 3 * u, :], ACT.Square).then_inc(s_sq, 1)
                    act_fn(qk[:, 0:INNER], ps[:, 3 * u, :], ACT.Copy).then_inc(s_qs, 1)
                    act.wait_ge(s_proj, 3 * T + 3)
                    after(act, s_vout[u], 8 * (T - u))
                    act_fn(v_tmp[:, u, :], ps[:, 3 * u + 2, :],
                           ACT.Copy).then_inc(s_vsv, 1)
                    act.wait_ge(s_ks, T + 1)
                    act_fn(sq[:, u, INNER:2 * INNER], qk[:, INNER:2 * INNER], ACT.Square).then_inc(s_sq, 1)
                tiles_in_pairs(act, 0, 2, TILES, TILES, project)
                act.wait_ge(s_nm, l + 1)
                act_fn(ssm[:], ssm[:], ACT.Sqrt).then_inc(s_nq, 1)

                def transposed(t, T, u):
                    act.wait_ge(s_tt, 2 * T + 1)
                    act_fn(kring[:, :, u:u + 3:2, :], ps[:, 0, :].rearrange("p (g a k) -> p g a k", g=PAIRS, a=2),
                           ACT.Copy).then_inc(s_kev, 1)
                    act.wait_ge(s_tt, 2 * T + 2)
                    for h, (a, b) in enumerate(HALVES):
                        ins = act_fn(qbd[a:b, :, :, h, :], ps[a:b, 1, :].rearrange("p (g w q) -> p g w q", g=PAIRS, w=2), ACT.Copy)
                        if h:
                            ins.then_inc(s_qev, 1)

                def exponentials(t, T, u):
                    act.wait_ge(s_sub, T + 1)
                    act_fn(sc, sc, ACT.Exp).then_inc(s_exp, 1)

                def outputs(t, T, u):
                    after(act, s_pv, T)
                    for b in range(2):
                        act.wait_ge(s_pt, 2 * T + b + 1)
                        act_fn(pt2[:, 512 * b:512 * (b + 1)], ps[:, 4 + b, :], ACT.Copy).then_inc(s_pte, 1)
                    act.wait_ge(s_pv, T + 1)
                    after(act, s_y, T)
                    for h, (a, b) in enumerate(HALVES):
                        o = ps[a:b, 6:8, :].rearrange("p b (g w h q) -> p (b g w) h q", g=2, w=2, h=2)
                        act_fn(ot[a:b].rearrange("p g (w q) -> p (g w) q", w=2), o[:, :, h, :], ACT.Copy).then_inc(s_oe, 1)

                def step(t, u):
                    T = TILES * l + t
                    if not (isinstance(t, int) and t >= TILES):
                        transposed(t, T, u)
                    if not (isinstance(t, int) and t < 1):
                        outputs(t - 1, T - 1, 1 - u)
                    if not (isinstance(t, int) and t >= TILES):
                        exponentials(t, T, u)
                tiles_in_pairs(act, 0, 2, TILES, TILES + 1, step)

                for j in range(GROUPS):
                    J = GROUPS * l + j
                    act.wait_ge(s_cp, J + 1)
                    act_fn(hc[:, GROUP * j:GROUP * (j + 1)], ps[:, j % 2, :], ACT.Copy).then_inc(s_hc, 1)
                    act_fn(sqf[:, GROUP * j:GROUP * (j + 1)], ps[:, j % 2, :], ACT.Square).then_inc(s_sqf, 1)
                act.wait_ge(s_vp2, GROUPS * (l + 1))
                act_fn(rs, ps[:, 2:6, :].rearrange("p b n -> p (b n)"), ACT.Ln, bias=eps[:, 0:1]).then_inc(s_ln, 1)
                act.wait_ge(s_ln, l + 1)
                act_fn(rs, rs, ACT.Exp, scale=-0.5).then_inc(s_rs, 1)
                for j in range(GROUPS):
                    J = GROUPS * l + j
                    for c, (o, m) in enumerate(CHUNKS):
                        act.wait_ge(s_g, 3 * J + c + 1)
                        after(act, s_gu, 3 * (J - 1) + c + 1)
                        act_fn(ge[0:m, GROUP * c:GROUP * (c + 1)], ps[0:m, 2 * c, :], ACT.Gelu,
                               bias=b1[0:m, l, 1, c:c + 1]).then_inc(s_ge, 1)
            act.wait_ge(s_ve, 2)
            act_fn(std[:], std[:], ACT.Sqrt).then_inc(s_sd, 1)

        @block.vector
        def _(dve):
            v = nc.vector
            v.memset(eps[:], EPS).then_inc(s_eps, 1)
            dve.wait_ge(s_rope, 32)
            for j in range(GROUPS):
                part = slice(GROUP * j, GROUP * (j + 1))
                for s, dst in enumerate((qt, kt)):
                    n = 2 * j + s
                    dve.wait_ge(s_qkp, n + 1)
                    after(dve, s_qkt, n)
                    for r in range(2):
                        v.tensor_tensor(rope_tmp[:, r, :], ps[:, 4 + 2 * (n % 2) + r, :], rope[:, r, part],
                                        ALU.mult).then_inc(s_rsn if r else s_rc, 1)
                    dve.wait_ge(s_rc, n + 1)
                    dve.wait_ge(s_rsn, n + 1)
                    v.tensor_tensor(dst[:, part], rope_tmp[:, 0, :], rope_tmp[:, 1, :], ALU.add).then_inc(s_qkt, 1)

            def maximum1(i):
                dve.wait_ge(s_s1, i + 1)
                after(dve, s_e1, i - 1)
                v.tensor_reduce(nmax[:, i % 2:i % 2 + 1], ps[:, 0:4, :].rearrange("p b n -> p (b n)")[:, 0:keys1(i)],
                                AX.X, ALU.max, negate=True).then_inc(s_m1, 1)
                dve.wait_ge(s_m1, i + 1)
                v.tensor_scalar(bias[:, i % 2:i % 2 + 1], nmax[:, i % 2:i % 2 + 1], SCALE1, None, ALU.mult).then_inc(s_b1, 1)

            def residual1(i):
                v.reciprocal(rinv[:, i % 2:i % 2 + 1], rsum[:, i % 2:i % 2 + 1]).then_inc(s_ri1, 1)
                dve.wait_ge(s_ri1, i + 1)
                dve.wait_ge(s_pv1, ends1[i])
                v.scalar_tensor_tensor(x_tok[:, i, :], ps[:, 6 + i % 2, 0:P], rinv[:, i % 2:i % 2 + 1], x_tok[:, i, :],
                                       ALU.mult, ALU.add).then_inc(s_o1, 1)
                dve.wait_ge(s_o1, i + 1)
                v.bn_stats(stats[:, i, :], x_tok[:, i, :]).then_inc(s_bs, 1)
                dve.wait_ge(s_bs, i + 1)
                v.bn_aggr(mean_var[:, i, :], stats[:, i, :]).then_inc(s_ba, 1)

            def inverse_std(n):
                dve.wait_ge(s_ba, TILES * n)
                v.tensor_scalar(std[:], mean_var[:, :, 1], EPS, None, ALU.add).then_inc(s_ve, 1)
                dve.wait_ge(s_sd, n)
                v.reciprocal(rstd[:], std[:]).then_inc(s_rd, 1)
                dve.wait_ge(s_rd, n)
            for i in range(TILES + 1):
                if i < TILES:
                    maximum1(i)
                if i:
                    dve.wait_ge(s_e1, i)
                    residual1(i - 1)
            inverse_std(1)
            for t in range(TILES):
                v.tensor_scalar(x_tok[:, t, :], x_tok[:, t, :], mean_var[:, t, 0:1], rstd[:, t:t + 1],
                                ALU.subtract, ALU.mult).then_inc(s_ln1, 1)
            for j in range(GROUPS):
                dve.wait_ge(s_x0p, j + 1)
                v.tensor_copy(x0[64:128, GROUP * j + 1:GROUP * (j + 1) + 1], ps[64:128, j, :]).then_inc(s_x0, 1)

            for l in range(DEPTH):
                src = xa if l else x0

                def project(t, u):
                    T = TILES * l + t
                    dve.wait_ge(s_proj, 3 * T + 2)
                    v.tensor_copy(qk_all[:, bass.ds(t, 1), HEADS:2 * HEADS, :].rearrange("p o h d -> p (o h d)"),
                                  ps[:, 3 * u + 1, :]).then_inc(s_ks, 1)
                    dve.wait_ge(s_sq, 2 * T + 2)
                    v.tensor_reduce(ss[:, bass.ds(t, 1), :].rearrange("p o h -> p (o h)"), sq[:, u, :].rearrange("p (h d) -> p h d", d=DH),
                                    AX.X, ALU.add).then_inc(s_ss, 1)
                tiles_in_pairs(dve, 0, 2, TILES, TILES, project)
                dve.wait_ge(s_ss, TILES * (l + 1))
                v.tensor_scalar(ssm[:], ss[:], 1e-24, None, ALU.max).then_inc(s_nm, 1)
                dve.wait_ge(s_nq, l + 1)
                v.reciprocal(rn[:], ssm[:]).then_inc(s_nr, 1)
                dve.wait_ge(s_nr, l + 1)
                dve.wait_ge(s_scaled, 3 * TILES * (l + 1))
                dve.wait_ge(s_qs, TILES * (l + 1))
                dve.wait_ge(s_ks, TILES * (l + 1))

                def front(t, T):
                    after(dve, s_tc, T)
                    after(dve, s_ts, 2 * T)
                    v.tensor_tensor(qn, qk_all[:, bass.ds(t, 1), :, :].rearrange("p o h d -> p (o h) d"),
                                    rn[:, bass.ds(t, 1), :].rearrange("p o h -> p (o h)")[:, :, None].to_broadcast([P, 2 * HEADS, DH]),
                                    ALU.mult).then_inc(s_qn, 1)
                    dve.wait_ge(s_qn, T + 1)
                    after(dve, s_qr, T)
                    qh, th = (z.rearrange("p (s h) d -> p s h d", s=2) for z in (qn, ts))
                    for h in range(2):
                        o, i = slice(32 * h, 32 * h + 32), slice(32 * (1 - h), 32 * (1 - h) + 32)
                        v.tensor_tensor(th[:, :, :, o], qh[:, :, :, i],
                                        scaled[:, 1, :, bass.ds(t, 1), o].to_broadcast([P, 2, HEADS, 32]),
                                        ALU.mult).then_inc(s_ts, 1)

                def rotate(t, T):
                    dve.wait_ge(s_ts, 2 * T + 2)
                    dve.wait_ge(s_tc, T + 1)
                    v.tensor_tensor(qr, tc.rearrange("p h d -> p (h d)"), ts.rearrange("p h d -> p (h d)"), ALU.add).then_inc(s_qr, 1)

                def shift_scores(t, T, u):
                    s3 = ps[:, 2:4, :].rearrange("p b (c k) -> p (b c) k", c=4)
                    dve.wait_ge(s_s, T + 1)
                    after(dve, s_sub, T)
                    v.tensor_reduce(smax[:], s3, AX.X, ALU.max).then_inc(s_mx, 1)
                    dve.wait_ge(s_mx, T + 1)
                    after(dve, s_pn, T)
                    v.tensor_tensor(sc.rearrange("p (c k) -> p c k", c=8), s3, smax[:, :, None].to_broadcast([P, 8, P]),
                                    ALU.subtract).then_inc(s_sub, 1)

                def sums(t, T, u):
                    dve.wait_ge(s_exp, T + 1)
                    after(dve, s_inv, T)
                    v.tensor_reduce(ssum[:], sc.rearrange("p (c k) -> p c k", c=8), AX.X, ALU.add).then_inc(s_sum, 1)
                    dve.wait_ge(s_sum, T + 1)
                    v.reciprocal(sinv[:], ssum[:]).then_inc(s_inv, 1)

                def residual(t, T):
                    dve.wait_ge(s_y, T + 1)
                    for h, (a, b) in enumerate(HALVES):
                        c = bass.ds(P * t + h, P)
                        v.tensor_tensor(xb[a:b, c], ps[a:b, 4, 0:P], src[a:b, c], ALU.add).then_inc(s_xb, 1)

                def step(t, u):
                    T = TILES * l + t
                    ahead = not (isinstance(t, int) and t + 1 >= TILES)
                    now = not (isinstance(t, int) and not 0 <= t < TILES)
                    if ahead:
                        front(t + 1, T + 1)
                    if now:
                        shift_scores(t, T, u)
                    if ahead:
                        rotate(t + 1, T + 1)
                    if now:
                        sums(t, T, u)
                    if not (isinstance(t, int) and t < 1):
                        residual(t - 1, T - 1)
                tiles_in_pairs(dve, -1, 2, TILES - 2, TILES + 1, step)

                dve.wait_ge(s_rs, l + 1)
                dve.wait_ge(s_wrest, 16 * 28)
                for j in range(GROUPS):
                    J = GROUPS * l + j
                    part = slice(GROUP * j, GROUP * (j + 1))
                    dve.wait_ge(s_hc, J + 1)
                    v.tensor_tensor(hn[:, part], hc[:, part], rs[:, part], ALU.mult).then_inc(s_hr, 1)
                    dve.wait_ge(s_hr, J + 1)
                    v.tensor_scalar(hn[:, part], hn[:, part], cols[:, l, 0:1], cols[:, l, 1:2], ALU.mult, ALU.add).then_inc(s_hn, 1)
                for j in range(GROUPS):
                    J = GROUPS * l + j
                    for c, (o, m) in enumerate(CHUNKS):
                        dve.wait_ge(s_a, 3 * J + c + 1)
                        dve.wait_ge(s_ge, 3 * J + c + 1)
                        after(dve, s_y2, J)
                        v.scalar_tensor_tensor(gu[0:m, GROUP * c:GROUP * (c + 1)], ps[0:m, 2 * c + 1, :], b1[0:m, l, 0, c:c + 1],
                                               ge[0:m, GROUP * c:GROUP * (c + 1)], ALU.add, ALU.mult).then_inc(s_gu, 1)
                    dve.wait_ge(s_y2, J + 1)
                    for h, (a, b) in enumerate(HALVES):
                        part = slice(GROUP * j + h, GROUP * (j + 1) + h)
                        v.scalar_tensor_tensor(xa[a:b, part], ps[a:b, 6, :], cols[a:b, l, 2:3], xb[a:b, part],
                                               ALU.add, ALU.add).then_inc(s_xf, 1)
                    if l == DEPTH - 1:
                        dve.wait_ge(s_xf, 2 * J + 2)
                        for h, (a, b) in enumerate(HALVES):
                            part = slice(GROUP * j + h, GROUP * (j + 1) + h)
                            v.tensor_tensor(fin[a:b, GROUP * j:GROUP * (j + 1)], xa[a:b, part], x0[a:b, part],
                                            ALU.add).then_inc(s_fs, 1)
            tile = lambda t: ps[:, t // 4, P * (t % 4):P * (t % 4 + 1)]
            for t in range(TILES):
                dve.wait_ge(s_ft, t // 4 + 1)
                v.bn_stats(stats[:, t, :], tile(t)).then_inc(s_bs, 1)
                dve.wait_ge(s_bs, TILES + t + 1)
                v.bn_aggr(mean_var[:, t, :], stats[:, t, :]).then_inc(s_ba, 1)
            inverse_std(2)
            for t in range(TILES):
                v.tensor_scalar(y_out[:, t, :], tile(t), mean_var[:, t, 0:1], rstd[:, t:t + 1],
                                ALU.subtract, ALU.mult).then_inc(s_fo, 1)


def rope_constants():
    i = np.arange(D // 2, dtype=np.float32)
    theta = np.power(np.float32(10000.0), (np.float32(-2.0) * i / np.float32(D)).astype(np.float32)).astype(np.float32)
    angle = np.arange(N, dtype=np.float32)[:, None] * theta[None, :]
    cos, sin = np.cos(angle).astype(np.float32), np.sin(angle).astype(np.float32)
    sign = np.where(np.arange(D) % 2 == 0, -1.0, 1.0).astype(np.float32)
    return np.ascontiguousarray(np.stack([np.repeat(cos, 2, 1).T, (np.repeat(sin, 2, 1) * sign).T]))


def xpos_constants():
    f = np.float32
    half = np.arange(0, DH, 2, dtype=f)
    inv = (f(1.0) / np.power(f(10000.0), half / f(DH))).astype(f)
    t = np.arange(N, dtype=f)
    freqs = t[:, None] * inv[None, :]
    base = (half + f(0.4 * DH)) / f(1.4 * DH)
    power = (t - f(N // 2)) / f(WINDOW // 2)
    scale = np.power(base[None, :], power[:, None]).astype(f)
    both = lambda a: np.concatenate([a, a], -1).astype(f)
    cos, sin, scale = both(np.cos(freqs)), both(np.sin(freqs)), both(scale)
    sign = np.where(np.arange(DH) < DH // 2, -1.0, 1.0).astype(f)
    return np.ascontiguousarray(np.stack([cos * scale * f(8), sin * scale * sign * f(8), cos / scale, sin / scale * sign]))


def kernel(L0_attn_x, L0_attn_Wq, L0_attn_Wk, L0_attn_Wv, L0_ffn_wqkv, L0_ffn_q_scale, L0_ffn_k_scale, L0_ffn_wo,
           L0_ffn_ln_g, L0_ffn_ln_b, L0_ffn_w1, L0_ffn_b1, L0_ffn_w2, L0_ffn_b2):
    import concourse.bacc as bacc
    from concourse.bass_utils import run_bass_kernel_spmd

    swap = np.arange(D) ^ 1
    wq, wk, wv = (np.asarray(w).T for w in (L0_attn_Wq, L0_attn_Wk, L0_attn_Wv))
    arrays = {
        "x": L0_attn_x,
        "w_qkv1": np.stack([wq, wq[:, swap], wk, wk[:, swap], wv]),
        "rope1": rope_constants(),
        "w_qkv": L0_ffn_wqkv, "q_scale": L0_ffn_q_scale, "k_scale": L0_ffn_k_scale, "w_o": L0_ffn_wo,
        "ln_g": L0_ffn_ln_g, "ln_b": L0_ffn_ln_b, "w_1": L0_ffn_w1, "b_1": L0_ffn_b1, "w_2": L0_ffn_w2, "b_2": L0_ffn_b2,
        "xpos": xpos_constants(),
    }
    nc = bacc.Bacc("TRN2", target_bir_lowering=False, num_devices=1)
    feeds, args = {}, []
    for name, a in arrays.items():
        a = np.ascontiguousarray(np.asarray(a))
        feeds[f"in_{name}"] = a
        args.append(nc.dram_tensor(f"in_{name}", a.shape, mybir.dt.from_np(a.dtype), kind="ExternalInput").ap())
    out = nc.dram_tensor("out", (1, N, D), mybir.dt.float32, kind="ExternalOutput").ap()
    build(nc, *args, out)
    r = run_bass_kernel_spmd(nc, [feeds], core_ids=[0])
    return r.results[0]["out"]
```

```python
import concourse.bass as bass
from concourse import mybir
from contextlib import ExitStack
import numpy as np

P = 128
N = 2048
TILES = N // P
D = 128
DEPTH = 2
HEADS = 8
DH = 64
PAIRS = HEADS // 2
WINDOW = 64
INNER = HEADS * DH
HID = int(D * 4 * 2 / 3)
CHUNKS = [(c, min(P, HID - c)) for c in range(0, HID, P)]
GROUP = 512
GROUPS = N // GROUP
NEG = -3.0e38
EPS = 1e-5
HALVES = ((0, 64), (64, 128))


def build(nc, x, w_qkv1, rope1, w_qkv, q_scale, k_scale, w_o, ln_g, ln_b, w_1, b_1, w_2, b_2, xpos, out):
    F = mybir.dt.float32
    BF = mybir.dt.bfloat16
    ALU = mybir.AluOpType
    ACT = mybir.ActivationFunctionType
    AX = mybir.AxisListType
    ctx = ExitStack()
    with ctx:
        def sb(name, shape, dt=F):
            return ctx.enter_context(nc.sbuf_tensor(name, shape, dt))

        def sem(name):
            return ctx.enter_context(nc.semaphore(name))

        ident = sb("ident", [P, P])
        ident_bf = sb("ident_bf", [P, P], BF)
        centre = sb("centre", [P, P])
        average = sb("average", [P, P])
        mask1 = sb("mask1", [P, P + 1], BF)
        mask2 = sb("mask2", [P, 2, 2, 2, WINDOW], BF)
        mask2_first = sb("mask2_first", [P, 2, 2, 2, WINDOW], BF)
        wqkv = sb("wqkv", [P, DEPTH, 3 * INNER])
        wo = sb("wo", [P, DEPTH, PAIRS, D])
        w1 = sb("w1", [P, DEPTH, 2 * HID])
        w2 = sb("w2", [P, DEPTH, len(CHUNKS), D])
        b1 = sb("b1", [P, DEPTH, 2, len(CHUNKS)])
        cols = sb("cols", [P, DEPTH, 3])
        table = sb("table", [P, 4, TILES, DH])
        qkscale = sb("qkscale", [P, DEPTH, 2, DH])
        scaled = sb("scaled", [P, 2, 2, TILES, DH])
        x0 = sb("x0", [P, N + 1])
        xa = sb("xa", [P, N + 1])
        xb = sb("xb", [P, N + 1])
        flat = scaled[:].rearrange("p a s t d -> p (a s t d)")
        x_tok = flat[:, 0:N].rearrange("p (t d) -> p t d", d=D)
        w1st = flat[:, N:N + 5 * P].rearrange("p (a e) -> p a e", a=5)
        qk_all = sb("qk_all", [P, TILES, 2 * HEADS, DH])
        arena = qk_all[:].rearrange("p t h d -> p (t h d)")
        rope = arena[:, 0:2 * N].rearrange("p (a n) -> p a n", a=2)
        xt, qt, kt = (arena[:, N * a:N * (a + 1)] for a in (2, 3, 4))
        v1 = arena[:, 5 * N:6 * N].rearrange("p (t d) -> p t d", d=D)
        vx = arena[0:1, 6 * N:7 * N].rearrange("p (t d) -> p t d", d=D)
        rope_tmp = arena[:, 7 * N:7 * N + 2 * GROUP].rearrange("p (a n) -> p a n", a=2)
        stats = sb("stats", [P, TILES, 6])
        mean_var = sb("mean_var", [P, TILES, 2])
        std = sb("std", [P, TILES])
        rstd = sb("rstd", [P, TILES])
        nmax = sb("nmax", [P, 2])
        bias = sb("bias", [P, 2])
        rsum = sb("rsum", [P, 2])
        rinv = sb("rinv", [P, 2])
        hs = sb("hs", [P, 2, P])
        v_tmp = sb("v_tmp", [P, 2, INNER])
        v_dram = nc.dram_tensor("v_dram", (TILES, P, INNER), F, kind="Internal").ap()
        ss = sb("ss", [P, TILES, 2 * HEADS])
        ssm = sb("ssm", [P, TILES, 2 * HEADS])
        rn = sb("rn", [P, TILES, 2 * HEADS])
        big = sb("big", [P, 7 * 1024])
        pbuf = big[:, 0:2 * N].rearrange("p (u n) -> p u n", u=2)
        ptb = big[:, 2 * N:2 * N + 1024].rearrange("p (b n) -> p b n", b=2)
        ptx = big[:, 2 * N + 1024:2 * N + 1152]
        sq = big[:, 0:2048].rearrange("p (u n) -> p u n", u=2)
        qn, ts, tc = (big[:, 1024 * a:1024 * (a + 1)].rearrange("p (h d) -> p h d", d=DH) for a in (0, 1, 2))
        qr, sc, pt2 = (big[:, 1024 * a:1024 * (a + 1)] for a in (2, 3, 4))
        pr = big[:, 5 * 1024:7 * 1024].rearrange("p (u n) -> p u n", u=2)
        qbd = sb("qbd", [P, PAIRS, 2, 2, WINDOW])
        kring = sb("kring", [P, PAIRS, 4, WINDOW])
        vs = sb("vs", [P, 2, INNER])
        vm = sb("vm", [P, 2, INNER])
        ot = sb("ot", [P, PAIRS, P])
        smax = sb("smax", [P, 8])
        ssum = sb("ssum", [P, 8])
        sinv = sb("sinv", [P, 8])
        eps = sb("eps", [P, 1])
        hc = qk_all[:, 0:2, :, :].rearrange("p t h d -> p (t h d)")
        rs = qk_all[:, 2:4, :, :].rearrange("p t h d -> p (t h d)")
        hn = qk_all[:, 4:6, :, :].rearrange("p t h d -> p (t h d)")
        sqf = qk_all[:, 6:8, :, :].rearrange("p t h d -> p (t h d)")
        ge = qk_all[:, 8:10, :, :].rearrange("p t h d -> p (t h d)")
        gu = qk_all[:, 10:12, :, :].rearrange("p t h d -> p (t h d)")
        fin = qk_all[:, 12:14, :, :].rearrange("p t h d -> p (t h d)")
        y_out = qk_all[:, 14:16, :, :].rearrange("p t h d -> p (t h d)").rearrange("p (t d) -> p t d", d=D)

        ps = ctx.enter_context(nc.psum_tensor("ps", [P, 8, 512], F))

        s_x, s_rope = [[sem(f"{n}_loaded_{j}") for j in range(GROUPS)] for n in ("x", "rope")]
        s_w1st, s_wqkv, s_wrest, s_tab = [sem(n) for n in ("w1st_loaded", "wqkv_loaded", "wrest_loaded", "tables_loaded")]
        s_const, s_cchain, s_scaled = sem("constants_made"), sem("constants_step"), sem("tables_scaled")
        s_xtp, s_xt = sem("xt_in_psum"), sem("xt_saved")
        s_qkp, s_rc, s_rsn, s_qkt = sem("qk_in_psum"), sem("rope_cos"), sem("rope_sin"), sem("qk_roped")
        s_vp, s_v = sem("v1_in_psum"), sem("v1_saved")
        s_vx = [sem(f"v1_rows_moved_{j}") for j in range(GROUPS)]
        s_s1, s_m1, s_b1, s_e1 = sem("scores1"), sem("max1"), sem("bias1"), sem("exp1")
        s_t1, s_pv1, s_ri1, s_o1 = sem("p1_transposed"), sem("out1"), sem("rinv1"), sem("res1")
        s_te1 = {"scalar": sem("pt1_saved_by_scalar"), "vector": sem("pt1_saved_by_vector")}
        s_bs, s_ba, s_sd, s_rd, s_ln1 = sem("bn_stats"), sem("bn_aggr"), sem("std_made"), sem("rstd_made"), sem("normed")
        s_ve, s_eps = sem("var_eps"), sem("eps_made")
        s_x0p, s_x0, s_xac = sem("x0_in_psum"), sem("x0_saved"), sem("xa_copied")
        s_hs, s_proj, s_sq, s_qs, s_vsv, s_ks, s_ss = [sem(n) for n in (
            "hs_staged", "qkv_in_psum", "squared", "q_saved", "v_saved", "k_saved", "sumsq_made")]
        s_nm, s_nq, s_nr = sem("norm_clipped"), sem("norm_rooted"), sem("norm_inverted")
        s_qn, s_tc, s_ts, s_qr = sem("qk_normed"), sem("times_cos"), sem("times_sin"), sem("qk_rotated")
        s_tt, s_kev, s_qev = sem("qk_transposed"), sem("kt_saved"), sem("qt_saved")
        s_s, s_mx, s_exp, s_inv, s_pn = [sem(n) for n in (
            "scores", "score_max", "score_exp", "exp_inv", "probs")]
        s_pt, s_pte, s_pv, s_oe, s_y, s_xb = [sem(n) for n in (
            "probs_transposed", "pt_saved", "pv_in_psum", "ot_saved", "attn_y", "xb_made")]
        s_vout = [sem("v_written_0"), sem("v_written_1")]
        s_vst = [sem("v_staged_0"), sem("v_staged_1")]
        s_cp, s_hc, s_sqf, s_vp2, s_ln, s_rs, s_hr, s_hn = [sem(n) for n in (
            "centred_in_psum", "centred_saved", "centred_squared", "var_in_psum", "var_log", "rstd_row", "hn_scaled", "hn_made")]
        s_g, s_a, s_ge, s_gu, s_y2, s_xf = [sem(n) for n in (
            "gate_in_psum", "value_in_psum", "gelu_made", "gated", "ffn_y", "ffn_out")]
        s_fs, s_ft, s_fo, s_out = sem("final_sum"), sem("final_in_psum"), sem("final_normed"), sem("out_written")

        def after(eng, semaphore, value):
            if not isinstance(value, int) or value > 0:
                eng.wait_ge(semaphore, value)

        def tiles_in_pairs(eng, first, loop_from, loop_to, last, step):
            for t in range(first, loop_from):
                step(t, t % 2)
            with eng.Fori(loop_from // 2, loop_to // 2) as pair:
                for u in range(2):
                    step(2 * pair + u, u)
            for t in range(loop_to, last):
                step(t, t % 2)

        def staged(l, t, u):
            layer = 16 * (3 * TILES // 2 - (1 - u))
            return layer * l + 24 * (t - u) + (48 if u else 32)

        def keys1(i):
            return min(P * (i + 1) + 1, N)

        LOTS = []
        ends1 = []
        by = {"scalar": 0, "vector": 0}
        for i in range(TILES):
            lots = [list(range(k, min(k + 4, i + 1))) for k in range(0, i + 1, 4)]
            lots += [None] * (keys1(i) > P * (i + 1))
            for n, keys in enumerate(lots):
                who = "scalar" if n < 2 else "vector"
                by[who] += 1
                LOTS.append((i, keys, who, by[who]))
            ends1.append(len(LOTS))

        def lots_of(i):
            return range(ends1[i - 1] if i else 0, ends1[i])

        def await_saved1(eng, lot):
            if lot >= 0:
                _, _, who, count = LOTS[lot]
                eng.wait_ge(s_te1[who], count)

        def save1(eng, copy, lot):
            _, keys, who, _ = LOTS[lot]
            eng.wait_ge(s_t1, lot + 1)
            after(eng, s_pv1, lot - 1)
            if keys is None:
                ins = copy(ptx[0:1, :], ps[0:1, 4 + lot % 2, 0:P])
            else:
                m = P * len(keys)
                ins = copy(ptb[:, lot % 2, 0:m], ps[:, 4 + lot % 2, 0:m])
            ins.then_inc(s_te1[who], 1)

        SCALE1 = 1.0 / float(np.sqrt(np.float32(D)))
        block = ctx.enter_context(nc.Block())

        @block.sync
        def _(sp):
            for j in range(GROUPS):
                sp.dma_start(x_tok[:, 4 * j:4 * j + 4, :], x.rearrange("b (t p) d -> p (b t) d", p=P)[:, 4 * j:4 * j + 4, :]).then_inc(s_x[j], 16)
                if j == 0:
                    sp.dma_start(w1st[:], w_qkv1.rearrange("a p e -> p a e")).then_inc(s_w1st, 16)
            for j in range(GROUPS):
                part = slice(GROUP * j, GROUP * (j + 1))
                sp.dma_start(rope[:, :, part], rope1.rearrange("a p n -> p a n")[:, :, part]).then_inc(s_rope[j], 16)
            sp.dma_start(wqkv[:], w_qkv.rearrange("l p n -> p l n")).then_inc(s_wqkv, 16)
            for s in range(4):
                sp.dma_start(table[:, s, :, :], xpos[s].rearrange("(t p) d -> p t d", p=P)).then_inc(s_tab, 16)
            for s, v in enumerate((q_scale, k_scale)):
                for l in range(DEPTH):
                    sp.dma_start(qkscale[:, l, s, :], v[l:l + 1, :].to_broadcast([P, DH])).then_inc(s_tab, 16)
            for l in range(DEPTH):
                sp.dma_start(wo[:, l], w_o[l].rearrange("(g p) n -> p g n", p=P)).then_inc(s_wrest, 16)
                sp.dma_start(w1[:, l], w_1[l]).then_inc(s_wrest, 16)
                for j, (c, m) in enumerate(CHUNKS):
                    sp.dma_start(w2[0:m, l, j, :], w_2[l, c:c + m, :]).then_inc(s_wrest, 16)
                    for ag in range(2):
                        sp.dma_start(b1[0:m, l, ag, j:j + 1],
                                     b_1[l, ag * HID + c:ag * HID + c + m].rearrange("(p o) -> p o", o=1)).then_inc(s_wrest, 16)
                for j, v in enumerate((ln_g, ln_b, b_2)):
                    sp.dma_start(cols[:, l, j:j + 1], v[l].rearrange("(p o) -> p o", o=1)).then_inc(s_wrest, 16)
            for j in range(GROUPS):
                sp.wait_ge(s_v, j + 1)
                sp.dma_start(vx[0:1, 4 * j:4 * j + 4, :], v1[0:1, 4 * j:4 * j + 4, :]).then_inc(s_vx[j], 16)
            for l in range(DEPTH):
                def write_v(t, u):
                    sp.wait_ge(s_vsv, TILES * l + t + 1)
                    sp.dma_start(v_dram[bass.ds(t, 1)].rearrange("o p n -> p (o n)"), v_tmp[:, u, :]).then_inc(s_vout[u], 16)
                tiles_in_pairs(sp, 0, 2, TILES, TILES, write_v)
                for u in range(2):
                    sp.wait_ge(s_vout[u], 8 * TILES * (l + 1))

                def stage(t, u):
                    T = TILES * l + t
                    after(sp, s_pv, T - 1)
                    sp.dma_start(vs[:, u, :], v_dram[bass.ds(t, 1)].rearrange("o p n -> p (o n)")).then_inc(s_vst[u], 16)
                    sp.dma_start(vm[0:64, u, :], v_dram[bass.ds(t, 1), 0:64].rearrange("o p n -> p (o n)")).then_inc(s_vst[u], 16)
                    if not (isinstance(t, int) and t == 0):
                        sp.dma_start(vm[64:128, u, :], v_dram[bass.ds(t - 1, 1), 64:128].rearrange("o p n -> p (o n)")).then_inc(s_vst[u], 16)
                tiles_in_pairs(sp, 0, 2, TILES, TILES, stage)
            for j in range(GROUPS):
                sp.wait_ge(s_fo, 4 * (j + 1))
                sp.dma_start(out.rearrange("b (t p) d -> p (b t) d", p=P)[:, 4 * j:4 * j + 4, :],
                             y_out[:, 4 * j:4 * j + 4, :]).then_inc(s_out, 16)
            sp.wait_ge(s_out, 16 * GROUPS)

        @block.gpsimd
        def _(pool):
            g = nc.gpsimd
            steps = [0]

            def chain(ins):
                steps[0] += 1
                ins.then_inc(s_cchain, 1)
                pool.wait_ge(s_cchain, steps[0])

            chain(g.memset(ident[:], 0.0))
            chain(g.affine_select(out=ident[:], in_=ident[:], compare_op=ALU.not_equal, fill=1.0, base=0,
                                  pattern=[[-1, P]], channel_multiplier=1))
            chain(g.tensor_copy(ident_bf[:], ident[:]))
            chain(g.memset(mask1[:], 0.0))
            chain(g.affine_select(out=mask1[:], in_=mask1[:], compare_op=ALU.is_ge, fill=NEG, base=1,
                                  pattern=[[-1, P + 1]], channel_multiplier=1))
            chain(g.memset(average[:], 1.0 / D))
            chain(g.tensor_scalar(centre[:], ident[:], -1.0 / D, None, ALU.add))
            for m in (mask2, mask2_first):
                chain(g.memset(m[:], 0.0))
                for a, b in HALVES:
                    for w in range(2):
                        for half in range(2):
                            own = half == w
                            v = m[a:b, :, w, half, :]
                            chain(g.affine_select(out=v, in_=v, compare_op=ALU.is_ge, fill=NEG, base=0,
                                                  pattern=[[0, 2], [-1 if own else 1, WINDOW]],
                                                  channel_multiplier=1 if own else -1))
            chain(g.memset(mask2_first[:, :, 0, 1, :], NEG))
            for buffer in (qbd, kring, vm):
                chain(g.memset(buffer[:], 0.0))
            for buffer in (x0, xa, xb):
                chain(g.memset(buffer[64:128, 0:1], 0.0))
            g.memset(x0[0:64, N:N + 1], 0.0).then_inc(s_const, 1)

            for l in range(DEPTH):
                if l == 0:
                    pool.wait_ge(s_tab, 16 * 8)
                src = xa if l else x0
                if l:
                    pool.wait_ge(s_xf, 2 * GROUPS * l)
                else:
                    pool.wait_ge(s_x0, 2 * GROUPS)

                def stage_h(t, u):
                    T = TILES * l + t
                    after(pool, s_proj, 3 * (T - 1))
                    g.tensor_copy(hs[:, u, :], src[:, bass.ds(P * t, P)]).then_inc(s_hs, 1)
                    row = bass.ds(t, 1)
                    g.tensor_tensor(scaled[:, 0, :, row, :].rearrange("p s o d -> p s (o d)"),
                                    table[:, 0:3:2, row, :].rearrange("p s o d -> p s (o d)"),
                                    qkscale[:, l], ALU.mult).then_inc(s_scaled, 1)
                    for h in range(2):
                        o, i = slice(32 * h, 32 * h + 32), slice(32 * (1 - h), 32 * (1 - h) + 32)
                        g.tensor_tensor(scaled[:, 1, :, row, o].rearrange("p s o d -> p s (o d)"),
                                        table[:, 1:4:2, row, o].rearrange("p s o d -> p s (o d)"),
                                        qkscale[:, l, :, i], ALU.mult).then_inc(s_scaled, 1)
                tiles_in_pairs(pool, 0, 2, TILES, TILES, stage_h)

                pool.wait_ge(s_scaled, 3 * TILES * (l + 1))

                def front(t, T):
                    pool.wait_ge(s_qn, T + 1)
                    after(pool, s_tt, 2 * T)
                    g.tensor_tensor(tc.rearrange("p (s h) d -> p s h d", s=2), qn.rearrange("p (s h) d -> p s h d", s=2),
                                    scaled[:, 0, :, bass.ds(t, 1), :].to_broadcast([P, 2, HEADS, DH]),
                                    ALU.mult).then_inc(s_tc, 1)

                def step(t, u):
                    T = TILES * l + t
                    if not (isinstance(t, int) and t + 1 >= TILES):
                        front(t + 1, T + 1)
                    if not (isinstance(t, int) and t < 0):
                        pool.wait_ge(s_inv, T + 1)
                        after(pool, s_pt, 2 * (T - 1))
                        g.tensor_tensor(pr[:, u, :].rearrange("p (b k) -> p b k", b=8), sc.rearrange("p (b k) -> p b k", b=8),
                                        sinv[:, :, None].to_broadcast([P, 8, P]), ALU.mult).then_inc(s_pn, 1)
                tiles_in_pairs(pool, -1, 2, TILES - 2, TILES, step)

        @block.tensor
        def _(pe):
            mm, tr = nc.tensor.matmul, nc.tensor.transpose
            pe.wait_ge(s_const, 1)
            for t in range(TILES):
                pe.wait_ge(s_x[t // 4], 16)
                ins = tr(ps[:, t // 4, P * (t % 4):P * (t % 4 + 1)], x_tok[:, t, :], ident[:])
                if t % 4 == 3:
                    ins.then_inc(s_xtp, 1)
            pe.wait_ge(s_w1st, 16)

            def project1(j):
                pe.wait_ge(s_xt, j + 1)
                after(pe, s_v, j)
                if j >= 2:
                    i = 4 * (j - 1)
                    for lot in lots_of(i - 2):
                        await_saved1(pe, lot)
                    pe.wait_ge(s_o1, i - 1)
                for s in range(2):
                    after(pe, s_rsn, 2 * j + s - 1)
                    for r in range(2):
                        ins = mm(ps[:, 4 + 2 * s + r, :], w1st[:, 2 * s + r, :], xt[:, GROUP * j:GROUP * (j + 1)],
                                 start=True, stop=True)
                    ins.then_inc(s_qkp, 1)
                pe.wait_ge(s_rsn, 2 * j + 1)
                for a in range(4):
                    t = 4 * j + a
                    ins = mm(ps[:, 4, P * a:P * (a + 1)], xt[:, P * t:P * (t + 1)], w1st[:, 4, :], start=True, stop=True)
                ins.then_inc(s_vp, 1)

            def scores1(i):
                pe.wait_ge(s_qkt, 2 * min(GROUPS, (i + 1) // 4 + 1))
                after(pe, s_e1, i)
                n = keys1(i)
                d, e = P * i, min(P * (i + 1), n)
                masked = (d // 512, (n - 1) // 512)
                for c in range(0, n, 512):
                    m = min(512, n - c)
                    mm(ps[:, c // 512, 0:m], qt[:, P * i:P * (i + 1)], kt[:, c:c + m], start=True,
                       stop=c // 512 not in masked, skip_group_check=True)
                ins = mm(ps[:, d // 512, d % 512:d % 512 + P], ident_bf[:], mask1[:, 0:P], start=False, stop=True, skip_group_check=True)
                if n > e:
                    ins = mm(ps[:, e // 512, e % 512:e % 512 + 1], ident_bf[:], mask1[:, P:P + 1], start=False, stop=True, skip_group_check=True)
                ins.then_inc(s_s1, 1)

            def transpose1(lot):
                i, keys, _, _ = LOTS[lot]
                await_saved1(pe, lot - 2)
                bank = 4 + lot % 2
                if keys is None:
                    ins = tr(ps[0:1, bank, 0:P], pbuf[:, i % 2, P * (i + 1):P * (i + 1) + 1], ident[:])
                else:
                    for a, k in enumerate(keys):
                        ins = tr(ps[:, bank, P * a:P * (a + 1)], pbuf[:, i % 2, P * k:P * (k + 1)], ident[:])
                ins.then_inc(s_t1, 1)

            def product1(lot):
                i, keys, _, _ = LOTS[lot]
                await_saved1(pe, lot)
                if keys is None:
                    pe.wait_ge(s_vx[(i + 1) // 4], 16)
                    ins = mm(ps[:, 6 + i % 2, 0:P], ptx[0:1, :], vx[0:1, i + 1, :], start=False, stop=True)
                else:
                    for a, k in enumerate(keys):
                        ins = mm(ps[:, 6 + i % 2, 0:P], ptb[:, lot % 2, P * a:P * (a + 1)], v1[:, k, :],
                                 start=k == 0, stop=lot == ends1[i] - 1 and a == len(keys) - 1)
                ins.then_inc(s_pv1, 1)

            def output1(i):
                pe.wait_ge(s_e1, i + 1)
                pe.wait_ge(s_v, i // 4 + 1)
                if i % 4 == 3 and i < TILES - 1:
                    pe.wait_ge(s_rsn, 2 * min(GROUPS, (i + 9) // 4))
                    pe.wait_ge(s_v, min(GROUPS, (i + 9) // 4))
                if i == 0:
                    pe.wait_ge(s_rsn, 4)
                    pe.wait_ge(s_v, 2)
                after(pe, s_o1, i - 1)
                lots = list(lots_of(i))
                transpose1(lots[0])
                for lot in lots:
                    if lot != lots[-1]:
                        transpose1(lot + 1)
                    product1(lot)
            for j in range(2):
                project1(j)
            for i in range(TILES + 1):
                if i < TILES:
                    scores1(i)
                if i and i % 4 == 0 and i // 4 + 1 < GROUPS:
                    project1(i // 4 + 1)
                if i:
                    output1(i - 1)
            for t in range(TILES):
                pe.wait_ge(s_ln1, t + 1)
                ins = tr(ps[:, t // 4, P * (t % 4):P * (t % 4 + 1)], x_tok[:, t, :], ident[:])
                if t % 4 == 3:
                    ins.then_inc(s_x0p, 1)

            for l in range(DEPTH):
                pe.wait_ge(s_wqkv, 16)
                if l == 0:
                    pe.wait_ge(s_x0, 2 * GROUPS)

                def project(t, u):
                    T = TILES * l + t
                    pe.wait_ge(s_hs, T + 1)
                    after(pe, s_vsv, T - 1)
                    after(pe, s_ks, T - 1)
                    for a in range(3):
                        mm(ps[:, 3 * u + a, :], hs[:, u, :], wqkv[:, l, INNER * a:INNER * (a + 1)], start=True, stop=True).then_inc(s_proj, 1)
                tiles_in_pairs(pe, 0, 2, TILES, TILES, project)
                pe.wait_ge(s_vsv, TILES * (l + 1))
                pe.wait_ge(s_ks, TILES * (l + 1))
                pe.wait_ge(s_wrest, 16 * 28)

                def transposes(t, T, u):
                    pe.wait_ge(s_qr, T + 1)
                    after(pe, s_qev, T)
                    for s, bank in ((1, 0), (0, 1)):
                        for g in range(PAIRS):
                            c = INNER * s + P * g
                            ins = tr(ps[:, bank, P * g:P * (g + 1)], qr[:, c:c + P], ident[:])
                        ins.then_inc(s_tt, 1)

                def scores(t, T, u):
                    after(pe, s_exp, 8 * T)
                    first = isinstance(t, int) and t == 0
                    for b in range(2):
                        mm(ps[:, 2 + b, :], ident_bf[:], (mask2_first if first else mask2)[:].rearrange("p g w a k -> p (g w a k)"),
                           start=True, stop=False, skip_group_check=True)
                    pe.wait_ge(s_kev, T + 1)
                    pe.wait_ge(s_qev, T + 1)
                    even = kring[:, :, 0:4:3, :] if u == 0 else kring[:, :, 1:3, :]
                    odd = kring[:, :, u:u + 3:2, :]
                    for g in range(PAIRS):
                        for w, keys in enumerate((even, odd)):
                            c = 256 * (g % 2) + P * w
                            ins = mm(ps[:, 2 + g // 2, c:c + P], qbd[:, g, w].rearrange("p h q -> p (h q)"), keys[:, g],
                                     start=False, stop=True, skip_group_check=True)
                    ins.then_inc(s_s, 1)

                def outputs(t, T, u):
                    pe.wait_ge(s_pn, T + 1)
                    after(pe, s_xb, 2 * T)
                    for b in range(2):
                        for a in range(4):
                            c = 512 * b + P * a
                            ins = tr(ps[:, 4 + b, P * a:P * (a + 1)], pr[:, u, c:c + P], ident[:])
                        ins.then_inc(s_pt, 1)
                    pe.wait_ge(s_vst[u], staged(l, t, u))
                    after(pe, s_oe, 2 * T)
                    for b in range(2):
                        pe.wait_ge(s_pte, 2 * T + b + 1)
                        for a in range(4):
                            g, w = 2 * b + a // 2, a % 2
                            c = 512 * b + P * a
                            ins = mm(ps[:, 6 + b, P * a:P * (a + 1)], (vs if w else vm)[:, u, P * g:P * (g + 1)], pt2[:, c:c + P],
                                     start=True, stop=True)
                    ins.then_inc(s_pv, 1)

                def project_out(t, T):
                    pe.wait_ge(s_oe, 2 * T + 2)
                    for g in range(PAIRS):
                        ins = mm(ps[:, 4, 0:P], wo[:, l, g, :], ot[:, g, :], start=g == 0, stop=g == PAIRS - 1)
                    ins.then_inc(s_y, 1)

                def step(t, u):
                    T = TILES * l + t
                    exact = isinstance(t, int)
                    if not (exact and t >= TILES):
                        transposes(t, T, u)
                    if not (exact and t < 2):
                        project_out(t - 2, T - 2)
                    if not (exact and t >= TILES):
                        scores(t, T, u)
                    if not (exact and not 1 <= t <= TILES):
                        outputs(t - 1, T - 1, 1 - u)
                tiles_in_pairs(pe, 0, 2, TILES, TILES + 2, step)

                for j in range(GROUPS + 1):
                    if j < GROUPS:
                        J = GROUPS * l + j
                        pe.wait_ge(s_xb, 2 * (TILES * l + 4 * j + 4))
                        if j >= 2:
                            pe.wait_ge(s_sqf, J - 1)
                            pe.wait_ge(s_hc, J - 1)
                        mm(ps[:, j % 2, :], centre[:], xb[:, GROUP * j:GROUP * (j + 1)], start=True, stop=True).then_inc(s_cp, 1)
                    if j:
                        J = GROUPS * l + j - 1
                        pe.wait_ge(s_sqf, J + 1)
                        mm(ps[:, 2 + j - 1, :], average[:], sqf[:, GROUP * (j - 1):GROUP * j], start=True, stop=True).then_inc(s_vp2, 1)

                pe.wait_ge(s_ln, l + 1)
                for j in range(GROUPS):
                    J = GROUPS * l + j
                    pe.wait_ge(s_hn, J + 1)
                    for c, (o, m) in enumerate(CHUNKS):
                        after(pe, s_gu, 3 * (J - 1) + c + 1)
                        mm(ps[0:m, 2 * c, :], w1[:, l, HID + o:HID + o + m], hn[:, GROUP * j:GROUP * (j + 1)],
                           start=True, stop=True).then_inc(s_g, 1)
                        mm(ps[0:m, 2 * c + 1, :], w1[:, l, o:o + m], hn[:, GROUP * j:GROUP * (j + 1)],
                           start=True, stop=True).then_inc(s_a, 1)
                    after(pe, s_xf, 2 * J)
                    for c, (o, m) in enumerate(CHUNKS):
                        pe.wait_ge(s_gu, 3 * J + c + 1)
                        ins = mm(ps[:, 6, :], w2[0:m, l, c, :], gu[0:m, GROUP * c:GROUP * (c + 1)],
                                 start=c == 0, stop=c == len(CHUNKS) - 1)
                    ins.then_inc(s_y2, 1)
            for t in range(TILES):
                pe.wait_ge(s_fs, 2 * (t // 4 + 1))
                ins = tr(ps[:, t // 4, P * (t % 4):P * (t % 4 + 1)], fin[:, P * t:P * (t + 1)], ident[:])
                if t % 4 == 3:
                    ins.then_inc(s_ft, 1)

        @block.scalar
        def _(act):
            act_fn = nc.scalar.activation
            for j in range(GROUPS):
                act.wait_ge(s_xtp, j + 1)
                act_fn(xt[:, GROUP * j:GROUP * (j + 1)], ps[:, j, :], ACT.Copy).then_inc(s_xt, 1)

            def save_v1(j):
                act.wait_ge(s_vp, j + 1)
                act_fn(v1[:, 4 * j:4 * j + 4, :].rearrange("p t d -> p (t d)"), ps[:, 4, :], ACT.Copy).then_inc(s_v, 1)
            for j in range(2):
                save_v1(j)
            for i in range(TILES + 1):
                if i and i % 4 == 0 and i // 4 + 1 < GROUPS:
                    save_v1(i // 4 + 1)
                if i:
                    for lot in lots_of(i - 1)[:2]:
                        save1(act, lambda o, x: act_fn(o, x, ACT.Copy), lot)
                if i < TILES:
                    act.wait_ge(s_b1, i + 1)
                    if i >= 2:
                        act.wait_ge(s_t1, ends1[i - 2])
                        act.wait_ge(s_ri1, i - 1)
                    act_fn(pbuf[:, i % 2, 0:keys1(i)], ps[:, 0:4, :].rearrange("p b n -> p (b n)")[:, 0:keys1(i)], ACT.Exp,
                           bias=bias[:, i % 2:i % 2 + 1], scale=SCALE1, accum_out=rsum[:, i % 2:i % 2 + 1]).then_inc(s_e1, 1)
            act.wait_ge(s_ve, 1)
            act_fn(std[:], std[:], ACT.Sqrt).then_inc(s_sd, 1)
            for j in range(GROUPS):
                act.wait_ge(s_x0p, j + 1)
                act_fn(x0[0:64, GROUP * j:GROUP * (j + 1)], ps[0:64, j, :], ACT.Copy).then_inc(s_x0, 1)

            for l in range(DEPTH):
                def project(t, u):
                    T = TILES * l + t
                    qk = qk_all[:, bass.ds(t, 1), :, :].rearrange("p o h d -> p (o h d)")
                    act.wait_ge(s_proj, 3 * T + 1)
                    after(act, s_ss, T - 1)
                    act_fn(sq[:, u, 0:INNER], ps[:, 3 * u, :], ACT.Square).then_inc(s_sq, 1)
                    act_fn(qk[:, 0:INNER], ps[:, 3 * u, :], ACT.Copy).then_inc(s_qs, 1)
                    act.wait_ge(s_proj, 3 * T + 3)
                    after(act, s_vout[u], 8 * (T - u))
                    act_fn(v_tmp[:, u, :], ps[:, 3 * u + 2, :],
                           ACT.Copy).then_inc(s_vsv, 1)
                    act.wait_ge(s_ks, T + 1)
                    act_fn(sq[:, u, INNER:2 * INNER], qk[:, INNER:2 * INNER], ACT.Square).then_inc(s_sq, 1)
                tiles_in_pairs(act, 0, 2, TILES, TILES, project)
                act.wait_ge(s_nm, l + 1)
                act_fn(ssm[:], ssm[:], ACT.Sqrt).then_inc(s_nq, 1)

                def transposed(t, T, u):
                    act.wait_ge(s_tt, 2 * T + 1)
                    act_fn(kring[:, :, u:u + 3:2, :], ps[:, 0, :].rearrange("p (g a k) -> p g a k", g=PAIRS, a=2),
                           ACT.Copy).then_inc(s_kev, 1)
                    act.wait_ge(s_tt, 2 * T + 2)
                    for h, (a, b) in enumerate(HALVES):
                        ins = act_fn(qbd[a:b, :, :, h, :], ps[a:b, 1, :].rearrange("p (g w q) -> p g w q", g=PAIRS, w=2), ACT.Copy)
                        if h:
                            ins.then_inc(s_qev, 1)

                def exponentials(t, T, u):
                    act.wait_ge(s_mx, T + 1)
                    after(act, s_pn, T)
                    after(act, s_inv, T)
                    for c in range(8):
                        act_fn(sc[:, P * c:P * (c + 1)], ps[:, 2 + c // 4, P * (c % 4):P * (c % 4 + 1)], ACT.Exp,
                               bias=smax[:, c:c + 1], accum_out=ssum[:, c:c + 1]).then_inc(s_exp, 1)

                def save_pt(t, T, u):
                    after(act, s_pv, T)
                    for b in range(2):
                        act.wait_ge(s_pt, 2 * T + b + 1)
                        act_fn(pt2[:, 512 * b:512 * (b + 1)], ps[:, 4 + b, :], ACT.Copy).then_inc(s_pte, 1)

                def step(t, u):
                    T = TILES * l + t
                    exact = isinstance(t, int)
                    if not (exact and t >= TILES):
                        transposed(t, T, u)
                    if not (exact and t < 1):
                        save_pt(t - 1, T - 1, 1 - u)
                    if not (exact and t >= TILES):
                        exponentials(t, T, u)
                tiles_in_pairs(act, 0, 2, TILES, TILES + 1, step)

                for j in range(GROUPS):
                    J = GROUPS * l + j
                    act.wait_ge(s_cp, J + 1)
                    act_fn(hc[:, GROUP * j:GROUP * (j + 1)], ps[:, j % 2, :], ACT.Copy).then_inc(s_hc, 1)
                    act_fn(sqf[:, GROUP * j:GROUP * (j + 1)], ps[:, j % 2, :], ACT.Square).then_inc(s_sqf, 1)
                act.wait_ge(s_vp2, GROUPS * (l + 1))
                act_fn(rs, ps[:, 2:6, :].rearrange("p b n -> p (b n)"), ACT.Ln, bias=eps[:, 0:1]).then_inc(s_ln, 1)
                act.wait_ge(s_ln, l + 1)
                act_fn(rs, rs, ACT.Exp, scale=-0.5).then_inc(s_rs, 1)
                for j in range(GROUPS):
                    J = GROUPS * l + j
                    for c, (o, m) in enumerate(CHUNKS):
                        act.wait_ge(s_g, 3 * J + c + 1)
                        after(act, s_gu, 3 * (J - 1) + c + 1)
                        act_fn(ge[0:m, GROUP * c:GROUP * (c + 1)], ps[0:m, 2 * c, :], ACT.Gelu,
                               bias=b1[0:m, l, 1, c:c + 1]).then_inc(s_ge, 1)
            act.wait_ge(s_ve, 2)
            act_fn(std[:], std[:], ACT.Sqrt).then_inc(s_sd, 1)

        @block.vector
        def _(dve):
            v = nc.vector
            v.memset(eps[:], EPS).then_inc(s_eps, 1)

            def rope1_chunk(j):
                part = slice(GROUP * j, GROUP * (j + 1))
                dve.wait_ge(s_rope[j], 16)
                for s, dst in enumerate((qt, kt)):
                    n = 2 * j + s
                    dve.wait_ge(s_qkp, n + 1)
                    after(dve, s_qkt, n)
                    for r in range(2):
                        v.tensor_tensor(rope_tmp[:, r, :], ps[:, 4 + 2 * s + r, :], rope[:, r, part],
                                        ALU.mult).then_inc(s_rsn if r else s_rc, 1)
                    dve.wait_ge(s_rc, n + 1)
                    dve.wait_ge(s_rsn, n + 1)
                    v.tensor_tensor(dst[:, part], rope_tmp[:, 0, :], rope_tmp[:, 1, :], ALU.add).then_inc(s_qkt, 1)

            def maximum1(i):
                dve.wait_ge(s_s1, i + 1)
                after(dve, s_e1, i - 1)
                v.tensor_reduce(nmax[:, i % 2:i % 2 + 1], ps[:, 0:4, :].rearrange("p b n -> p (b n)")[:, 0:keys1(i)],
                                AX.X, ALU.max, negate=True).then_inc(s_m1, 1)
                dve.wait_ge(s_m1, i + 1)
                v.tensor_scalar(bias[:, i % 2:i % 2 + 1], nmax[:, i % 2:i % 2 + 1], SCALE1, None, ALU.mult).then_inc(s_b1, 1)

            def residual1(i):
                v.reciprocal(rinv[:, i % 2:i % 2 + 1], rsum[:, i % 2:i % 2 + 1]).then_inc(s_ri1, 1)
                dve.wait_ge(s_ri1, i + 1)
                dve.wait_ge(s_pv1, ends1[i])
                v.scalar_tensor_tensor(x_tok[:, i, :], ps[:, 6 + i % 2, 0:P], rinv[:, i % 2:i % 2 + 1], x_tok[:, i, :],
                                       ALU.mult, ALU.add).then_inc(s_o1, 1)
                dve.wait_ge(s_o1, i + 1)
                v.bn_stats(stats[:, i, :], x_tok[:, i, :]).then_inc(s_bs, 1)
                dve.wait_ge(s_bs, i + 1)
                v.bn_aggr(mean_var[:, i, :], stats[:, i, :]).then_inc(s_ba, 1)

            def inverse_std(n):
                dve.wait_ge(s_ba, TILES * n)
                v.tensor_scalar(std[:], mean_var[:, :, 1], EPS, None, ALU.add).then_inc(s_ve, 1)
                dve.wait_ge(s_sd, n)
                v.reciprocal(rstd[:], std[:]).then_inc(s_rd, 1)
                dve.wait_ge(s_rd, n)
            for j in range(2):
                rope1_chunk(j)
            for i in range(TILES + 1):
                if i < TILES:
                    maximum1(i)
                if i and i % 4 == 0 and i // 4 + 1 < GROUPS:
                    rope1_chunk(i // 4 + 1)
                if i:
                    for lot in lots_of(i - 1)[2:]:
                        save1(dve, v.tensor_copy, lot)
                    dve.wait_ge(s_e1, i)
                    residual1(i - 1)
            inverse_std(1)
            for t in range(TILES):
                v.tensor_scalar(x_tok[:, t, :], x_tok[:, t, :], mean_var[:, t, 0:1], rstd[:, t:t + 1],
                                ALU.subtract, ALU.mult).then_inc(s_ln1, 1)
            for j in range(GROUPS):
                dve.wait_ge(s_x0p, j + 1)
                v.tensor_copy(x0[64:128, GROUP * j + 1:GROUP * (j + 1) + 1], ps[64:128, j, :]).then_inc(s_x0, 1)

            for l in range(DEPTH):
                src = xa if l else x0

                def project(t, u):
                    T = TILES * l + t
                    dve.wait_ge(s_proj, 3 * T + 2)
                    v.tensor_copy(qk_all[:, bass.ds(t, 1), HEADS:2 * HEADS, :].rearrange("p o h d -> p (o h d)"),
                                  ps[:, 3 * u + 1, :]).then_inc(s_ks, 1)
                    dve.wait_ge(s_sq, 2 * T + 2)
                    v.tensor_reduce(ss[:, bass.ds(t, 1), :].rearrange("p o h -> p (o h)"), sq[:, u, :].rearrange("p (h d) -> p h d", d=DH),
                                    AX.X, ALU.add).then_inc(s_ss, 1)
                tiles_in_pairs(dve, 0, 2, TILES, TILES, project)
                dve.wait_ge(s_ss, TILES * (l + 1))
                v.tensor_scalar(ssm[:], ss[:], 1e-24, None, ALU.max).then_inc(s_nm, 1)
                dve.wait_ge(s_nq, l + 1)
                v.reciprocal(rn[:], ssm[:]).then_inc(s_nr, 1)
                dve.wait_ge(s_nr, l + 1)
                dve.wait_ge(s_scaled, 3 * TILES * (l + 1))
                dve.wait_ge(s_qs, TILES * (l + 1))
                dve.wait_ge(s_ks, TILES * (l + 1))

                def front(t, T):
                    after(dve, s_tc, T)
                    after(dve, s_ts, 2 * T)
                    v.tensor_tensor(qn, qk_all[:, bass.ds(t, 1), :, :].rearrange("p o h d -> p (o h) d"),
                                    rn[:, bass.ds(t, 1), :].rearrange("p o h -> p (o h)")[:, :, None].to_broadcast([P, 2 * HEADS, DH]),
                                    ALU.mult).then_inc(s_qn, 1)
                    dve.wait_ge(s_qn, T + 1)
                    after(dve, s_qr, T)
                    qh, th = (z.rearrange("p (s h) d -> p s h d", s=2) for z in (qn, ts))
                    for h in range(2):
                        o, i = slice(32 * h, 32 * h + 32), slice(32 * (1 - h), 32 * (1 - h) + 32)
                        v.tensor_tensor(th[:, :, :, o], qh[:, :, :, i],
                                        scaled[:, 1, :, bass.ds(t, 1), o].to_broadcast([P, 2, HEADS, 32]),
                                        ALU.mult).then_inc(s_ts, 1)

                def rotate(t, T):
                    dve.wait_ge(s_ts, 2 * T + 2)
                    dve.wait_ge(s_tc, T + 1)
                    v.tensor_tensor(qr, tc.rearrange("p h d -> p (h d)"), ts.rearrange("p h d -> p (h d)"), ALU.add).then_inc(s_qr, 1)

                def maximum(t, T, u):
                    s3 = ps[:, 2:4, :].rearrange("p b (c k) -> p (b c) k", c=4)
                    dve.wait_ge(s_s, T + 1)
                    v.tensor_reduce(smax[:], s3, AX.X, ALU.max, negate=True).then_inc(s_mx, 1)

                def invert_sums(t, T, u):
                    dve.wait_ge(s_exp, 8 * T + 8)
                    after(dve, s_pn, T)
                    v.reciprocal(sinv[:], ssum[:]).then_inc(s_inv, 1)

                def save_out(t, T, u):
                    dve.wait_ge(s_pv, T + 1)
                    after(dve, s_y, T)
                    for h, (a, b) in enumerate(HALVES):
                        o = ps[a:b, 6:8, :].rearrange("p b (g w h q) -> p (b g w) h q", g=2, w=2, h=2)
                        v.tensor_copy(ot[a:b].rearrange("p g (w q) -> p (g w) q", w=2), o[:, :, h, :]).then_inc(s_oe, 1)

                def residual(t, T):
                    dve.wait_ge(s_y, T + 1)
                    for h, (a, b) in enumerate(HALVES):
                        c = bass.ds(P * t + h, P)
                        v.tensor_tensor(xb[a:b, c], ps[a:b, 4, 0:P], src[a:b, c], ALU.add).then_inc(s_xb, 1)

                def step(t, u):
                    T = TILES * l + t
                    exact = isinstance(t, int)
                    ahead = not (exact and t + 1 >= TILES)
                    now = not (exact and not 0 <= t < TILES)
                    if not (exact and t < 2):
                        residual(t - 2, T - 2)
                    if ahead:
                        front(t + 1, T + 1)
                    if now:
                        maximum(t, T, u)
                    if ahead:
                        rotate(t + 1, T + 1)
                    if not (exact and not 1 <= t <= TILES):
                        save_out(t - 1, T - 1, 1 - u)
                    if now:
                        invert_sums(t, T, u)
                tiles_in_pairs(dve, -1, 2, TILES - 2, TILES + 2, step)

                dve.wait_ge(s_rs, l + 1)
                dve.wait_ge(s_wrest, 16 * 28)
                for j in range(GROUPS):
                    J = GROUPS * l + j
                    part = slice(GROUP * j, GROUP * (j + 1))
                    dve.wait_ge(s_hc, J + 1)
                    v.tensor_tensor(hn[:, part], hc[:, part], rs[:, part], ALU.mult).then_inc(s_hr, 1)
                    dve.wait_ge(s_hr, J + 1)
                    v.tensor_scalar(hn[:, part], hn[:, part], cols[:, l, 0:1], cols[:, l, 1:2], ALU.mult, ALU.add).then_inc(s_hn, 1)
                for j in range(GROUPS):
                    J = GROUPS * l + j
                    for c, (o, m) in enumerate(CHUNKS):
                        dve.wait_ge(s_a, 3 * J + c + 1)
                        dve.wait_ge(s_ge, 3 * J + c + 1)
                        after(dve, s_y2, J)
                        v.scalar_tensor_tensor(gu[0:m, GROUP * c:GROUP * (c + 1)], ps[0:m, 2 * c + 1, :], b1[0:m, l, 0, c:c + 1],
                                               ge[0:m, GROUP * c:GROUP * (c + 1)], ALU.add, ALU.mult).then_inc(s_gu, 1)
                    dve.wait_ge(s_y2, J + 1)
                    for h, (a, b) in enumerate(HALVES):
                        part = slice(GROUP * j + h, GROUP * (j + 1) + h)
                        v.scalar_tensor_tensor(xa[a:b, part], ps[a:b, 6, :], cols[a:b, l, 2:3], xb[a:b, part],
                                               ALU.add, ALU.add).then_inc(s_xf, 1)
                    if l == DEPTH - 1:
                        dve.wait_ge(s_xf, 2 * J + 2)
                        for h, (a, b) in enumerate(HALVES):
                            part = slice(GROUP * j + h, GROUP * (j + 1) + h)
                            v.tensor_tensor(fin[a:b, GROUP * j:GROUP * (j + 1)], xa[a:b, part], x0[a:b, part],
                                            ALU.add).then_inc(s_fs, 1)
            tile = lambda t: ps[:, t // 4, P * (t % 4):P * (t % 4 + 1)]
            for t in range(TILES):
                dve.wait_ge(s_ft, t // 4 + 1)
                v.bn_stats(stats[:, t, :], tile(t)).then_inc(s_bs, 1)
                dve.wait_ge(s_bs, TILES + t + 1)
                v.bn_aggr(mean_var[:, t, :], stats[:, t, :]).then_inc(s_ba, 1)
            inverse_std(2)
            for t in range(TILES):
                v.tensor_scalar(y_out[:, t, :], tile(t), mean_var[:, t, 0:1], rstd[:, t:t + 1],
                                ALU.subtract, ALU.mult).then_inc(s_fo, 1)


def rope_constants():
    i = np.arange(D // 2, dtype=np.float32)
    theta = np.power(np.float32(10000.0), (np.float32(-2.0) * i / np.float32(D)).astype(np.float32)).astype(np.float32)
    angle = np.arange(N, dtype=np.float32)[:, None] * theta[None, :]
    cos, sin = np.cos(angle).astype(np.float32), np.sin(angle).astype(np.float32)
    sign = np.where(np.arange(D) % 2 == 0, -1.0, 1.0).astype(np.float32)
    return np.ascontiguousarray(np.stack([np.repeat(cos, 2, 1).T, (np.repeat(sin, 2, 1) * sign).T]))


def xpos_constants():
    f = np.float32
    half = np.arange(0, DH, 2, dtype=f)
    inv = (f(1.0) / np.power(f(10000.0), half / f(DH))).astype(f)
    t = np.arange(N, dtype=f)
    freqs = t[:, None] * inv[None, :]
    base = (half + f(0.4 * DH)) / f(1.4 * DH)
    power = (t - f(N // 2)) / f(WINDOW // 2)
    scale = np.power(base[None, :], power[:, None]).astype(f)
    both = lambda a: np.concatenate([a, a], -1).astype(f)
    cos, sin, scale = both(np.cos(freqs)), both(np.sin(freqs)), both(scale)
    sign = np.where(np.arange(DH) < DH // 2, -1.0, 1.0).astype(f)
    return np.ascontiguousarray(np.stack([cos * scale * f(8), sin * scale * sign * f(8), cos / scale, sin / scale * sign]))


def kernel(L0_attn_x, L0_attn_Wq, L0_attn_Wk, L0_attn_Wv, L0_ffn_wqkv, L0_ffn_q_scale, L0_ffn_k_scale, L0_ffn_wo,
           L0_ffn_ln_g, L0_ffn_ln_b, L0_ffn_w1, L0_ffn_b1, L0_ffn_w2, L0_ffn_b2):
    import concourse.bacc as bacc
    from concourse.bass_utils import run_bass_kernel_spmd

    swap = np.arange(D) ^ 1
    wq, wk, wv = (np.asarray(w).T for w in (L0_attn_Wq, L0_attn_Wk, L0_attn_Wv))
    arrays = {
        "x": L0_attn_x,
        "w_qkv1": np.stack([wq, wq[:, swap], wk, wk[:, swap], wv]),
        "rope1": rope_constants(),
        "w_qkv": L0_ffn_wqkv, "q_scale": L0_ffn_q_scale, "k_scale": L0_ffn_k_scale, "w_o": L0_ffn_wo,
        "ln_g": L0_ffn_ln_g, "ln_b": L0_ffn_ln_b, "w_1": L0_ffn_w1, "b_1": L0_ffn_b1, "w_2": L0_ffn_w2, "b_2": L0_ffn_b2,
        "xpos": xpos_constants(),
    }
    nc = bacc.Bacc("TRN2", target_bir_lowering=False, num_devices=1)
    feeds, args = {}, []
    for name, a in arrays.items():
        a = np.ascontiguousarray(np.asarray(a))
        feeds[f"in_{name}"] = a
        args.append(nc.dram_tensor(f"in_{name}", a.shape, mybir.dt.from_np(a.dtype), kind="ExternalInput").ap())
    out = nc.dram_tensor("out", (1, N, D), mybir.dt.float32, kind="ExternalOutput").ap()
    build(nc, *args, out)
    r = run_bass_kernel_spmd(nc, [feeds], core_ids=[0])
    return r.results[0]["out"]
```

```python
import concourse.bass as bass
from concourse import mybir
from contextlib import ExitStack
import numpy as np

P = 128
N = 2048
TILES = N // P
D = 128
DEPTH = 2
HEADS = 8
DH = 64
PAIRS = HEADS // 2
WINDOW = 64
INNER = HEADS * DH
HID = int(D * 4 * 2 / 3)
CHUNKS = [(c, min(P, HID - c)) for c in range(0, HID, P)]
GROUP = 512
GROUPS = N // GROUP
AHEAD = 5
NEG = -3.0e38
EPS = 1e-5
FFN_NORM_PARTS = ((1, 0, 4), (2, 4, 8), (3, 8, 12), (4, 12, 15), (5, 15, 16))
QK_NORM_PARTS = (slice(0, 2), slice(2, 16))
HALVES = ((0, 64), (64, 128))


def build(nc, x, w_qkv1, rope1, w_qkv, q_scale, k_scale, w_o, ln_g, ln_b, w_1, b_1, w_2, b_2, xpos, out):
    F = mybir.dt.float32
    R = mybir.dt.float32r
    BF = mybir.dt.bfloat16
    ALU = mybir.AluOpType
    ACT = mybir.ActivationFunctionType
    AX = mybir.AxisListType
    ctx = ExitStack()
    with ctx:
        def sb(name, shape, dt=F):
            return ctx.enter_context(nc.sbuf_tensor(name, shape, dt))

        def sem(name):
            return ctx.enter_context(nc.semaphore(name))

        ident = sb("ident", [P, P])
        ident_bf = sb("ident_bf", [P, P], BF)
        centre = sb("centre", [P, P])
        average = sb("average", [P, P])
        mask1 = sb("mask1", [P, P + 1], BF)
        mask2 = sb("mask2", [P, 2, 2, 2, WINDOW], BF)
        mask2_first = sb("mask2_first", [P, 2, 2, 2, WINDOW], BF)
        wqkv = sb("wqkv", [P, 3 * INNER])
        wqkv_hi, wqkv_lo = (sb(f"wqkv_{n}", [P, 3 * INNER], R) for n in ("hi", "lo"))
        w1_hi, w1_lo = (sb(f"w1_{n}", [P, 2 * HID], R) for n in ("hi", "lo"))
        w2_hi, w2_lo = (sb(f"w2_{n}", [P, len(CHUNKS), D], R) for n in ("hi", "lo"))
        wo = sb("wo", [P, DEPTH, PAIRS, D])
        w1 = sb("w1", [P, DEPTH, 2 * HID])
        w2 = sb("w2", [P, DEPTH, len(CHUNKS), D])
        b1 = sb("b1", [P, DEPTH, 2, len(CHUNKS)])
        cols = sb("cols", [P, DEPTH, 3])
        qkscale = sb("qkscale", [P, DEPTH, 2, DH])
        scaled = sb("scaled", [P, 2, 2, TILES, DH])
        x0 = sb("x0", [P, N + 1])
        xa = sb("xa", [P, N + 1])
        xb = sb("xb", [P, N + 1])
        flat = scaled[:].rearrange("p a s t d -> p (a s t d)")
        x_tok = flat[:, 0:N].rearrange("p (t d) -> p t d", d=D)
        w1st = flat[:, N:N + 5 * P].rearrange("p (a e) -> p a e", a=5)
        qk_all = sb("qk_all", [P, TILES, 2 * HEADS, DH])
        arena_at = nc.sbuf_base - 4 * TILES * 2 * INNER
        arena = qk_all[:].rearrange("p t h d -> p (t h d)")
        rope = arena[:, 0:2 * N].rearrange("p (a n) -> p a n", a=2)
        xt = arena[:, 2 * N:3 * N]
        v1 = arena[:, 5 * N:6 * N].rearrange("p (t d) -> p t d", d=D)
        vx = xb[0:1, 0:N].rearrange("p (t d) -> p t d", d=D)
        stats = sb("stats", [P, TILES, 6])
        mean_var = sb("mean_var", [P, TILES, 2])
        std = sb("std", [P, TILES])
        rstd = sb("rstd", [P, TILES])
        nmax = sb("nmax", [P, 2])
        bias = sb("bias", [P, 2])
        rsum = sb("rsum", [P, 2])
        rinv = sb("rinv", [P, 2])
        hs_hi, hs_lo = (sb(f"hs_{n}", [P, 2, P], R) for n in ("hi", "lo"))
        v_tmp = sb("v_tmp", [P, 2, INNER])
        v_dram = nc.dram_tensor("v_dram", (TILES, P, INNER), F, kind="Internal").ap()
        ss = sb("ss", [P, TILES, 2 * HEADS])
        ssm = sb("ssm", [P, TILES, 2 * HEADS])
        rn = sb("rn", [P, TILES, 2 * HEADS])
        big = sb("big", [P, 7 * 1024])
        pbuf = big[:, 0:2 * N].rearrange("p (u n) -> p u n", u=2)
        ptb = big[:, 2 * N:2 * N + 1024].rearrange("p (b n) -> p b n", b=2)
        ptx = big[:, 2 * N + 1024:2 * N + 1152]
        sq = big[:, 5 * 1024:7 * 1024].rearrange("p (u n) -> p u n", u=2)
        qn, ts, tc = (big[:, 1024 * a:1024 * (a + 1)].rearrange("p (h d) -> p h d", d=DH) for a in (0, 1, 2))
        qr, pt2, pr = (big[:, 1024 * a:1024 * (a + 1)] for a in (2, 4, 6))
        sc = [big[:, 1024 * a:1024 * (a + 1)] for a in (3, 5)]
        qbd = sb("qbd", [P, PAIRS, 2, 2, WINDOW])
        kring = sb("kring", [P, PAIRS, 4, WINDOW])
        vs = sb("vs", [P, 2, INNER])
        vm = sb("vm", [P, 2, INNER])
        ot = sb("ot", [P, PAIRS, P])
        smax = sb("smax", [P, 8])
        ssum = sb("ssum", [P, 8])
        sinv = sb("sinv", [P, 8])
        eps = sb("eps", [P, 1])
        hc, rs, hn, sqf = (arena[:, N * a:N * (a + 1)] for a in range(4))
        ge, gu = big[:, 0:len(CHUNKS) * GROUP], big[:, N:N + len(CHUNKS) * GROUP]
        hn_hi, hn_lo, gu_hi, gu_lo = (nc.alloc_sbuf_tensor_at(f"{n}", [P, N], R, offset=arena_at + 4 * N * (4 + a))
                                      for a, n in enumerate(("hn_hi", "hn_lo", "gu_hi", "gu_lo")))
        qt_hi = nc.alloc_sbuf_tensor_at("qt_hi", [P, N], R, offset=arena_at + 4 * N * 3)
        kt_hi, qt_lo, kt_lo = hn_hi, gu_hi, gu_lo
        rope_tmp, roped = vs, v_tmp
        fin = arena[:, 0:N]
        y_out = arena[:, N:2 * N].rearrange("p (t d) -> p t d", d=D)

        ps = ctx.enter_context(nc.psum_tensor("ps", [P, 8, 512], F))

        s_x, s_rope = [[sem(f"{n}_loaded_{j}") for j in range(GROUPS)] for n in ("x", "rope")]
        s_w1st, s_wqkv, s_wrest, s_tab, s_qks = [sem(n) for n in (
            "w1st_loaded", "wqkv_loaded", "wrest_loaded", "tables_loaded", "qkscale_loaded")]
        s_id, s_const, s_cchain, s_scaled = sem("ident_made"), sem("constants_made"), sem("constants_step"), sem("tables_scaled")
        s_xtp, s_xt = sem("xt_in_psum"), sem("xt_saved")
        s_qkp, s_rc, s_rsn, s_qkt = sem("qk_in_psum"), sem("rope_cos"), sem("rope_sin"), sem("qk_roped")
        s_qkh, s_qkl = sem("qk_hi_made"), sem("qk_lo_made")
        s_vp, s_v = sem("v1_in_psum"), sem("v1_saved")
        s_vx = [sem(f"v1_rows_moved_{j}") for j in range(GROUPS)]
        s_s1, s_m1, s_b1, s_e1 = sem("scores1"), sem("max1"), sem("bias1"), sem("exp1")
        s_t1, s_pv1, s_ri1, s_o1 = sem("p1_transposed"), sem("out1"), sem("rinv1"), sem("res1")
        s_te1 = {"scalar": sem("pt1_saved_by_scalar"), "vector": sem("pt1_saved_by_vector")}
        s_bs, s_ba, s_sd, s_rd, s_ln1 = sem("bn_stats"), sem("bn_aggr"), sem("std_made"), sem("rstd_made"), sem("normed")
        s_ve, s_eps = sem("var_eps"), sem("eps_made")
        s_x0p, s_x0a, s_x0v = sem("x0_in_psum"), sem("x0_saved_by_scalar"), sem("x0_saved_by_vector")
        s_hs, s_hl, s_proj, s_sq, s_qs, s_vsv, s_ks, s_ss = [sem(n) for n in (
            "hs_high_staged", "hs_low_staged", "qkv_in_psum", "squared", "q_saved", "v_saved", "k_saved", "sumsq_made")]
        s_nm, s_nq, s_nr = sem("norm_clipped"), sem("norm_rooted"), sem("norm_inverted")
        s_qn, s_tc, s_ts, s_qr = sem("qk_normed"), sem("times_cos"), sem("times_sin"), sem("qk_rotated")
        s_tt, s_kev, s_qev = sem("qk_transposed"), sem("kt_saved"), sem("qt_saved")
        s_s, s_mx, s_exp, s_inv, s_pn = [sem(n) for n in (
            "scores", "score_max", "score_exp", "exp_inv", "probs")]
        s_pt, s_pte, s_pv, s_oe, s_y, s_xb = [sem(n) for n in (
            "probs_transposed", "pt_saved", "pv_in_psum", "ot_saved", "attn_y", "xb_made")]
        s_vout = [sem("v_written_0"), sem("v_written_1")]
        s_vst = [sem("v_staged_0"), sem("v_staged_1")]
        s_cp, s_hc, s_sqf, s_vp2, s_ln, s_rs, s_hr, s_hn = [sem(n) for n in (
            "centred_in_psum", "centred_saved", "centred_squared", "var_in_psum", "var_log", "rstd_row", "hn_scaled", "hn_made")]
        s_g, s_a, s_ge, s_gu, s_y2, s_xf = [sem(n) for n in (
            "gate_in_psum", "value_in_psum", "gelu_made", "gated", "ffn_y", "ffn_out")]
        s_wsplit, s_wq, s_w12, s_nhi, s_nlo, s_ghi, s_glo = [sem(n) for n in (
            "weight_hi", "wqkv_split", "w12_split", "hn_hi_made", "hn_lo_made", "gated_hi", "gated_lo")]
        s_fs, s_fs3, s_fcopy = sem("final_sum"), sem("final_sum_of_last_group"), sem("final_copied")
        s_ft, s_fo, s_out = sem("final_in_psum"), sem("final_normed"), sem("out_written")

        def after(eng, semaphore, value):
            if not isinstance(value, int) or value > 0:
                eng.wait_ge(semaphore, value)

        def tiles_in_pairs(eng, first, loop_from, loop_to, last, step):
            for t in range(first, loop_from):
                step(t, t % 2)
            with eng.Fori(loop_from // 2, loop_to // 2) as pair:
                for u in range(2):
                    step(2 * pair + u, u)
            for t in range(loop_to, last):
                step(t, t % 2)

        def norm_part(n):
            bank, a, b = FFN_NORM_PARTS[n]
            return ps[:, bank, P * (a % 4):P * (a % 4) + P * (b - a)]

        def staged(l, t, u):
            layer = 16 * (3 * TILES // 2 - (1 - u))
            return layer * l + 24 * (t - u) + (48 if u else 32)

        def keys1(i):
            return min(P * (i + 1) + 1, N)

        LOTS = []
        ends1 = []
        by = {"scalar": 0, "vector": 0}
        for i in range(TILES):
            lots = [list(range(k, min(k + 4, i + 1))) for k in range(0, i + 1, 4)]
            lots += [None] * (keys1(i) > P * (i + 1))
            for n, keys in enumerate(lots):
                who = "scalar" if n < 2 else "vector"
                by[who] += 1
                LOTS.append((i, keys, who, by[who]))
            ends1.append(len(LOTS))

        def lots_of(i):
            return range(ends1[i - 1] if i else 0, ends1[i])

        def await_saved1(eng, lot):
            if lot >= 0:
                _, _, who, count = LOTS[lot]
                eng.wait_ge(s_te1[who], count)

        def save1(eng, copy, lot):
            _, keys, who, _ = LOTS[lot]
            eng.wait_ge(s_t1, lot + 1)
            after(eng, s_pv1, lot - 1)
            if keys is None:
                ins = copy(ptx[0:1, :], ps[0:1, 4 + lot % 2, 0:P])
            else:
                m = P * len(keys)
                ins = copy(ptb[:, lot % 2, 0:m], ps[:, 4 + lot % 2, 0:m])
            ins.then_inc(s_te1[who], 1)

        SCALE1 = 1.0 / float(np.sqrt(np.float32(D)))
        block = ctx.enter_context(nc.Block())

        @block.sync
        def _(sp):
            for j in range(GROUPS):
                sp.dma_start(x_tok[:, 4 * j:4 * j + 4, :], x.rearrange("b (t p) d -> p (b t) d", p=P)[:, 4 * j:4 * j + 4, :]).then_inc(s_x[j], 16)
                if j == 0:
                    sp.dma_start(w1st[:], w_qkv1.rearrange("a p e -> p a e")).then_inc(s_w1st, 16)
            for j in range(GROUPS):
                part = slice(GROUP * j, GROUP * (j + 1))
                sp.dma_start(rope[:, :, part], rope1.rearrange("a p n -> p a n")[:, :, part]).then_inc(s_rope[j], 16)
            sp.dma_start(wqkv[:], w_qkv[0]).then_inc(s_wqkv, 16)
            for s, v in enumerate((q_scale, k_scale)):
                for l in range(DEPTH):
                    sp.dma_start(qkscale[:, l, s, :], v[l:l + 1, :].to_broadcast([P, DH])).then_inc(s_qks, 16)
            for l in range(DEPTH):
                sp.dma_start(wo[:, l], w_o[l].rearrange("(g p) n -> p g n", p=P)).then_inc(s_wrest, 16)
                sp.dma_start(w1[:, l], w_1[l]).then_inc(s_wrest, 16)
                for j, (c, m) in enumerate(CHUNKS):
                    sp.dma_start(w2[0:m, l, j, :], w_2[l, c:c + m, :]).then_inc(s_wrest, 16)
                    for ag in range(2):
                        sp.dma_start(b1[0:m, l, ag, j:j + 1],
                                     b_1[l, ag * HID + c:ag * HID + c + m].rearrange("(p o) -> p o", o=1)).then_inc(s_wrest, 16)
                for j, v in enumerate((ln_g, ln_b, b_2)):
                    sp.dma_start(cols[:, l, j:j + 1], v[l].rearrange("(p o) -> p o", o=1)).then_inc(s_wrest, 16)
            for j in range(GROUPS):
                sp.wait_ge(s_v, j + 1)
                sp.dma_start(vx[0:1, 4 * j:4 * j + 4, :], v1[0:1, 4 * j:4 * j + 4, :]).then_inc(s_vx[j], 16)
            def load_tables():
                for c in range(2):
                    for s in range(2):
                        sp.dma_start(scaled[:, c, s], xpos[c, s].rearrange("(t p) d -> p t d", p=P)).then_inc(s_tab, 16)
            sp.wait_ge(s_x0p, GROUPS)
            load_tables()
            for l in range(DEPTH):
                def write_v(t, u):
                    sp.wait_ge(s_vsv, TILES * l + t + 1)
                    sp.dma_start(v_dram[bass.ds(t, 1)].rearrange("o p n -> p (o n)"), v_tmp[:, u, :]).then_inc(s_vout[u], 16)
                tiles_in_pairs(sp, 0, 2, TILES, TILES, write_v)
                for u in range(2):
                    sp.wait_ge(s_vout[u], 8 * TILES * (l + 1))

                def stage(t, u):
                    T = TILES * l + t
                    after(sp, s_pv, T - 1)
                    sp.dma_start(vs[:, u, :], v_dram[bass.ds(t, 1)].rearrange("o p n -> p (o n)")).then_inc(s_vst[u], 16)
                    sp.dma_start(vm[0:64, u, :], v_dram[bass.ds(t, 1), 0:64].rearrange("o p n -> p (o n)")).then_inc(s_vst[u], 16)
                    if not (isinstance(t, int) and t == 0):
                        sp.dma_start(vm[64:128, u, :], v_dram[bass.ds(t - 1, 1), 64:128].rearrange("o p n -> p (o n)")).then_inc(s_vst[u], 16)
                if l + 1 < DEPTH:
                    sp.wait_ge(s_wq, l + 1)
                    sp.dma_start(wqkv[:], w_qkv[l + 1]).then_inc(s_wqkv, 16)
                tiles_in_pairs(sp, 0, 2, TILES, TILES, stage)
                if l + 1 < DEPTH:
                    sp.wait_ge(s_qr, TILES * (l + 1))
                    load_tables()
            for j in range(GROUPS):
                sp.wait_ge(s_fo, 4 * (j + 1))
                sp.dma_start(out.rearrange("b (t p) d -> p (b t) d", p=P)[:, 4 * j:4 * j + 4, :],
                             y_out[:, 4 * j:4 * j + 4, :]).then_inc(s_out, 16)
            sp.wait_ge(s_out, 16 * GROUPS)

        @block.gpsimd
        def _(pool):
            g = nc.gpsimd
            steps = [0]

            def chain(ins):
                steps[0] += 1
                ins.then_inc(s_cchain, 1)
                pool.wait_ge(s_cchain, steps[0])

            chain(g.memset(ident[:], 0.0))
            chain(g.affine_select(out=ident[:], in_=ident[:], compare_op=ALU.not_equal, fill=1.0, base=0,
                                  pattern=[[-1, P]], channel_multiplier=1))
            chain(g.tensor_copy(ident_bf[:], ident[:]))
            g.memset(x0[0:64, N:N + 1], 0.0).then_inc(s_id, 1)
            pool.wait_ge(s_id, 1)
            chain(g.memset(mask1[:], 0.0))
            chain(g.affine_select(out=mask1[:], in_=mask1[:], compare_op=ALU.is_ge, fill=NEG, base=1,
                                  pattern=[[-1, P + 1]], channel_multiplier=1))
            chain(g.memset(average[:], 1.0 / D))
            chain(g.tensor_scalar(centre[:], ident[:], -1.0 / D, None, ALU.add))
            for m in (mask2, mask2_first):
                chain(g.memset(m[:], 0.0))
                for a, b in HALVES:
                    for w in range(2):
                        for half in range(2):
                            own = half == w
                            v = m[a:b, :, w, half, :]
                            chain(g.affine_select(out=v, in_=v, compare_op=ALU.is_ge, fill=NEG, base=0,
                                                  pattern=[[0, 2], [-1 if own else 1, WINDOW]],
                                                  channel_multiplier=1 if own else -1))
            chain(g.memset(mask2_first[:, :, 0, 1, :], NEG))
            for buffer in (qbd, kring, vm):
                chain(g.memset(buffer[:], 0.0))
            for buffer in (xa, xb):
                chain(g.memset(buffer[64:128, 0:1], 0.0))
            g.memset(x0[64:128, 0:1], 0.0).then_inc(s_const, 1)
            pool.wait_ge(s_const, 1)

            splits = [0]

            def split(hi, lo, w, semaphore):
                g.tensor_copy(hi, w).then_inc(s_wsplit, 1)
                splits[0] += 1
                pool.wait_ge(s_wsplit, splits[0])
                g.tensor_tensor(lo, w, hi.bitcast(F), ALU.subtract).then_inc(semaphore, 1)

            def split_wqkv(l):
                pool.wait_ge(s_wqkv, 16 * (l + 1))
                after(pool, s_proj, 3 * TILES * l)
                split(wqkv_hi[:], wqkv_lo[:], wqkv[:], s_wq)

            def split_w12(l):
                pool.wait_ge(s_wrest, 16 * 28)
                after(pool, s_y2, GROUPS * l)
                split(w1_hi[:], w1_lo[:], w1[:, l], s_w12)
                for c, (o, m) in enumerate(CHUNKS):
                    split(w2_hi[0:m, c], w2_lo[0:m, c], w2[0:m, l, c], s_w12)
            def qk_low(j):
                for s, (hi, lo) in enumerate(((qt_hi, qt_lo), (kt_hi, kt_lo))):
                    part = slice(GROUP * j, GROUP * (j + 1))
                    pool.wait_ge(s_qkh, 2 * j + s + 1)
                    g.tensor_tensor(lo[:, part], roped[:, s, :], hi[:, part].bitcast(F), ALU.subtract).then_inc(s_qkl, 1)
            for j in range(2):
                qk_low(j)
            split_wqkv(0)
            split_w12(0)
            for j in range(2, GROUPS):
                qk_low(j)
            pool.wait_ge(s_qks, 64)
            for l in range(DEPTH):
                src = xa if l else x0

                def stage_h(t, u):
                    T = TILES * l + t
                    if l == 0 and isinstance(t, int) and t in (0, 2):
                        pool.wait_ge(s_x0a, 2 * t or 1)
                        pool.wait_ge(s_x0v, 2 * t or 1)
                    if l and isinstance(t, int) and t in (0, 2):
                        pool.wait_ge(s_xf, 2 * (GROUPS * (l - 1) + (2 * t or 1)))
                    after(pool, s_proj, 3 * (T - 1))
                    g.tensor_copy(hs_hi[:, u, :], src[:, bass.ds(P * t, P)]).then_inc(s_hs, 1)

                def scale_tables(t):
                    row = bass.ds(t, 1)
                    cos, sin = (scaled[:, c, :, row, :].rearrange("p s o d -> p s (o d)") for c in range(2))
                    g.tensor_tensor(cos, cos, qkscale[:, l], ALU.mult).then_inc(s_scaled, 1)
                    for h in range(2):
                        o, i = slice(32 * h, 32 * h + 32), slice(32 * (1 - h), 32 * (1 - h) + 32)
                        g.tensor_tensor(sin[:, :, o], sin[:, :, o], qkscale[:, l, :, i], ALU.mult).then_inc(s_scaled, 1)
                stage_h(0, 0)
                stage_h(1, 1)
                stage_h(2, 0)
                stage_h(3, 1)
                tiles_in_pairs(pool, 4, 4, TILES - 4, TILES - 4, stage_h)
                pool.wait_ge(s_tab, 64 * (l + 1))
                for t in range(4):
                    stage_h(TILES - 4 + t, t % 2)
                    if t < 3:
                        scale_tables(t)


                def front(t, T):
                    pool.wait_ge(s_scaled, 3 * T + 3)
                    pool.wait_ge(s_qn, T + 1)
                    after(pool, s_tt, 2 * T)
                    g.tensor_tensor(tc.rearrange("p (s h) d -> p s h d", s=2), qn.rearrange("p (s h) d -> p s h d", s=2),
                                    scaled[:, 0, :, bass.ds(t, 1), :].to_broadcast([P, 2, HEADS, DH]),
                                    ALU.mult).then_inc(s_tc, 1)

                for t in range(2):
                    front(t, TILES * l + t)
                    scale_tables(t + 3)

                def step(t, u):
                    T = TILES * l + t
                    if not (isinstance(t, int) and t + 2 >= TILES):
                        front(t + 2, T + 2)
                    if not (isinstance(t, int) and t < 0):
                        pool.wait_ge(s_inv, T + 1)
                        after(pool, s_pt, 2 * T)
                        g.tensor_tensor(pr.rearrange("p (b k) -> p b k", b=8), sc[u].rearrange("p (b k) -> p b k", b=8),
                                        sinv[:, :, None].to_broadcast([P, 8, P]), ALU.mult).then_inc(s_pn, 1)
                        if not (isinstance(t, int) and t + AHEAD >= TILES):
                            scale_tables(t + AHEAD)
                tiles_in_pairs(pool, 0, 2, TILES - AHEAD - 1, TILES, step)

                if l + 1 < DEPTH:
                    split_wqkv(l + 1)
                if l:
                    split_w12(l)
                for j in range(GROUPS):
                    part = slice(GROUP * j, GROUP * (j + 1))
                    pool.wait_ge(s_nhi, GROUPS * l + j + 1)
                    g.tensor_tensor(hn_lo[:, part], hn[:, part], hn_hi[:, part].bitcast(F), ALU.subtract).then_inc(s_nlo, 1)
            pool.wait_ge(s_nlo, GROUPS * DEPTH)
            for j in range(GROUPS - 1):
                pool.wait_ge(s_xf, 2 * (GROUPS * (DEPTH - 1) + j + 1))
                for h, (a, b) in enumerate(HALVES):
                    after(pool, s_fs, 2 * j + h)
                    part = slice(GROUP * j + h, GROUP * (j + 1) + h)
                    g.tensor_tensor(fin[a:b, GROUP * j:GROUP * (j + 1)], xa[a:b, part], x0[a:b, part],
                                    ALU.add).then_inc(s_fs, 1)

        @block.tensor
        def _(pe):
            mm, tr = nc.tensor.matmul, nc.tensor.transpose
            pe.wait_ge(s_id, 1)
            for t in range(TILES):
                pe.wait_ge(s_x[t // 4], 16)
                ins = tr(ps[:, t // 4, P * (t % 4):P * (t % 4 + 1)], x_tok[:, t, :], ident[:])
                if t % 4 == 3:
                    ins.then_inc(s_xtp, 1)
            pe.wait_ge(s_w1st, 16)

            def project1(j):
                pe.wait_ge(s_xt, j + 1)
                after(pe, s_v, j)
                if j >= 2:
                    i = 4 * (j - 1)
                    for lot in lots_of(i - 2):
                        await_saved1(pe, lot)
                    pe.wait_ge(s_o1, i - 1)
                for s in range(2):
                    after(pe, s_rsn, 2 * j + s - 1)
                    for r in range(2):
                        ins = mm(ps[:, 4 + 2 * s + r, :], w1st[:, 2 * s + r, :], xt[:, GROUP * j:GROUP * (j + 1)],
                                 start=True, stop=True)
                    ins.then_inc(s_qkp, 1)
                pe.wait_ge(s_rsn, 2 * j + 1)
                for a in range(4):
                    t = 4 * j + a
                    ins = mm(ps[:, 4, P * a:P * (a + 1)], xt[:, P * t:P * (t + 1)], w1st[:, 4, :], start=True, stop=True)
                ins.then_inc(s_vp, 1)

            def scores1(i):
                if i == 0:
                    pe.wait_ge(s_const, 1)
                pe.wait_ge(s_qkl, 2 * min(GROUPS, (i + 1) // 4 + 1))
                after(pe, s_e1, i)
                n = keys1(i)
                d, e = P * i, min(P * (i + 1), n)
                masked = (d // 512, (n - 1) // 512)
                for c in range(0, n, 512):
                    m = min(512, n - c)
                    m += m % 2
                    q, k = (qt_hi[:, P * i:P * (i + 1)], qt_lo[:, P * i:P * (i + 1)]), (kt_hi[:, c:c + m], kt_lo[:, c:c + m])
                    for n_part, (a, b) in enumerate(((0, 0), (0, 1), (1, 0))):
                        mm(ps[:, c // 512, 0:m], q[a], k[b], start=n_part == 0,
                           stop=n_part == 2 and c // 512 not in masked, skip_group_check=True)
                ins = mm(ps[:, d // 512, d % 512:d % 512 + P], ident_bf[:], mask1[:, 0:P], start=False, stop=True, skip_group_check=True)
                if n > e:
                    ins = mm(ps[:, e // 512, e % 512:e % 512 + 1], ident_bf[:], mask1[:, P:P + 1], start=False, stop=True, skip_group_check=True)
                ins.then_inc(s_s1, 1)

            def transpose1(lot):
                i, keys, _, _ = LOTS[lot]
                await_saved1(pe, lot - 2)
                bank = 4 + lot % 2
                if keys is None:
                    ins = tr(ps[0:1, bank, 0:P], pbuf[:, i % 2, P * (i + 1):P * (i + 1) + 1], ident[:])
                else:
                    for a, k in enumerate(keys):
                        ins = tr(ps[:, bank, P * a:P * (a + 1)], pbuf[:, i % 2, P * k:P * (k + 1)], ident[:])
                ins.then_inc(s_t1, 1)

            def product1(lot):
                i, keys, _, _ = LOTS[lot]
                await_saved1(pe, lot)
                if keys is None:
                    pe.wait_ge(s_vx[(i + 1) // 4], 16)
                    ins = mm(ps[:, 6 + i % 2, 0:P], ptx[0:1, :], vx[0:1, i + 1, :], start=False, stop=True)
                else:
                    for a, k in enumerate(keys):
                        ins = mm(ps[:, 6 + i % 2, 0:P], ptb[:, lot % 2, P * a:P * (a + 1)], v1[:, k, :],
                                 start=k == 0, stop=lot == ends1[i] - 1 and a == len(keys) - 1)
                ins.then_inc(s_pv1, 1)

            def start_output1(i):
                pe.wait_ge(s_e1, i + 1)
                pe.wait_ge(s_v, i // 4 + 1)
                if i % 4 == 3 and i < TILES - 1:
                    pe.wait_ge(s_rsn, 2 * min(GROUPS, (i + 9) // 4))
                    pe.wait_ge(s_v, min(GROUPS, (i + 9) // 4))
                if i == 0:
                    pe.wait_ge(s_rsn, 4)
                    pe.wait_ge(s_v, 2)
                for lot in list(lots_of(i))[:2]:
                    transpose1(lot)

            def finish_output1(i):
                after(pe, s_o1, i - 1)
                lots = list(lots_of(i))
                for n, lot in enumerate(lots):
                    if n >= 1 and n + 1 < len(lots):
                        transpose1(lot + 1)
                    product1(lot)
            for j in range(2):
                project1(j)
            for i in range(TILES + 1):
                projecting = i and i % 4 == 0 and i // 4 + 1 < GROUPS
                if projecting:
                    project1(i // 4 + 1)
                elif i:
                    start_output1(i - 1)
                if i < TILES:
                    scores1(i)
                if projecting:
                    start_output1(i - 1)
                if i:
                    finish_output1(i - 1)
            await_saved1(pe, len(LOTS) - 1)
            await_saved1(pe, len(LOTS) - 2)
            for t in range(TILES):
                pe.wait_ge(s_ln1, t + 1)
                ins = tr(ps[:, 4 + t // 4, P * (t % 4):P * (t % 4 + 1)], x_tok[:, t, :], ident[:])
                if t % 4 == 3:
                    ins.then_inc(s_x0p, 1)

            for l in range(DEPTH):
                pe.wait_ge(s_wq, l + 1)

                def project(t, u):
                    T = TILES * l + t
                    if l == 0 and isinstance(t, int) and t == 1:
                        pe.wait_ge(s_x0a, 2)
                        pe.wait_ge(s_x0v, 2)
                    pe.wait_ge(s_hs, T + 1)
                    pe.wait_ge(s_hl, T + 1)
                    after(pe, s_vsv, T - 1)
                    after(pe, s_ks, T - 1)
                    for a in range(3):
                        part = slice(INNER * a, INNER * (a + 1))
                        mm(ps[:, 3 * u + a, :], hs_hi[:, u, :], wqkv_hi[:, part], start=True, stop=False)
                        mm(ps[:, 3 * u + a, :], hs_hi[:, u, :], wqkv_lo[:, part], start=False, stop=False)
                        mm(ps[:, 3 * u + a, :], hs_lo[:, u, :], wqkv_hi[:, part], start=False, stop=True).then_inc(s_proj, 1)
                tiles_in_pairs(pe, 0, 2, TILES, TILES, project)
                pe.wait_ge(s_vsv, TILES * (l + 1) - 1)
                pe.wait_ge(s_ks, TILES * (l + 1) - 1)

                def transposes(t, T, u):
                    pe.wait_ge(s_qr, T + 1)
                    after(pe, s_qev, T)
                    after(pe, s_xb, 2 * (T - 3))
                    for s, bank in ((1, 0), (0, 1)):
                        for g in range(PAIRS):
                            c = INNER * s + P * g
                            ins = tr(ps[:, bank, P * g:P * (g + 1)], qr[:, c:c + P], ident[:])
                        ins.then_inc(s_tt, 1)

                def scores(t, T, u):
                    first = isinstance(t, int) and t == 0
                    if first:
                        pe.wait_ge(s_vsv, TILES * (l + 1))
                        pe.wait_ge(s_ks, TILES * (l + 1))
                    even = kring[:, :, 0:4:3, :] if u == 0 else kring[:, :, 1:3, :]
                    odd = kring[:, :, u:u + 3:2, :]
                    for b in range(2):
                        if not (isinstance(T, int) and T == 0):
                            pe.wait_ge(s_exp, 8 * T - 4 * (1 - b))
                        mm(ps[:, 2 + b, :], ident_bf[:], (mask2_first if first else mask2)[:].rearrange("p g w a k -> p (g w a k)"),
                           start=True, stop=False, skip_group_check=True)
                        if b == 0:
                            pe.wait_ge(s_kev, T + 1)
                            pe.wait_ge(s_qev, T + 1)
                        for g in (2 * b, 2 * b + 1):
                            for w, keys in enumerate((even, odd)):
                                c = 256 * (g % 2) + P * w
                                ins = mm(ps[:, 2 + b, c:c + P], qbd[:, g, w].rearrange("p h q -> p (h q)"), keys[:, g],
                                         start=False, stop=True, skip_group_check=True)
                        ins.then_inc(s_s, 1)

                def transpose_probs(t, T):
                    pe.wait_ge(s_pn, T + 1)
                    for b in range(2):
                        for a in range(4):
                            c = 512 * b + P * a
                            ins = tr(ps[:, 4 + b, P * a:P * (a + 1)], pr[:, c:c + P], ident[:])
                        ins.then_inc(s_pt, 1)

                def values(t, T, u):
                    pe.wait_ge(s_vst[u], staged(l, t, u))
                    after(pe, s_oe, 2 * T)
                    for b in range(2):
                        pe.wait_ge(s_pte, 2 * T + b + 1)
                        for a in range(4):
                            g, w = 2 * b + a // 2, a % 2
                            c = 512 * b + P * a
                            ins = mm(ps[:, 6 + b, P * a:P * (a + 1)], (vs if w else vm)[:, u, P * g:P * (g + 1)], pt2[:, c:c + P],
                                     start=True, stop=True)
                    ins.then_inc(s_pv, 1)

                def project_out(t, T, kept):
                    pe.wait_ge(s_kev, kept)
                    pe.wait_ge(s_oe, 2 * T + 2)
                    for g in range(PAIRS):
                        ins = mm(ps[:, 0, 0:P], wo[:, l, g, :], ot[:, g, :], start=g == 0, stop=g == PAIRS - 1)
                    ins.then_inc(s_y, 1)

                def centred(n):
                    _, a, b = FFN_NORM_PARTS[n]
                    pe.wait_ge(s_xb, 2 * (TILES * l + b))
                    mm(norm_part(n), centre[:], xb[:, P * a:P * b], start=True, stop=True).then_inc(s_cp, 1)

                def variance(n):
                    _, a, b = FFN_NORM_PARTS[n]
                    pe.wait_ge(s_sqf, len(FFN_NORM_PARTS) * l + n + 1)
                    pe.wait_ge(s_hc, len(FFN_NORM_PARTS) * l + n + 1)
                    mm(norm_part(n), average[:], sqf[:, P * a:P * b], start=True, stop=True).then_inc(s_vp2, 1)

                def step(t, u):
                    T = TILES * l + t
                    exact = isinstance(t, int)
                    ahead = not (exact and t + 1 >= TILES)
                    if not (exact and not 0 <= t < TILES):
                        scores(t, T, u)
                    if not (exact and t < 2):
                        values(t - 2, T - 2, u)
                    if ahead:
                        transposes(t + 1, T + 1, 1 - u)
                    if exact and t == TILES:
                        pe.wait_ge(s_qev, TILES * (l + 1))
                        centred(0)
                    if not (exact and not 1 <= t <= TILES):
                        transpose_probs(t - 1, T - 1)
                    if exact and t == TILES:
                        pe.wait_ge(s_exp, 8 * TILES * (l + 1))
                        centred(1)
                    if exact and t == TILES + 1:
                        variance(0)
                        variance(1)
                    if not (exact and t < 2):
                        project_out(t - 2, T - 2, T + 2 if ahead else TILES * (l + 1))
                    if exact and t == TILES + 1:
                        variance(2)
                        centred(3)
                    if exact and t == TILES:
                        centred(2)
                tiles_in_pairs(pe, -1, 2, TILES - 2, TILES + 2, step)
                centred(4)
                variance(3)
                variance(4)

                pe.wait_ge(s_ln, len(FFN_NORM_PARTS) * (l + 1))
                def one_pass(o, w, x, start, stop):
                    mm(o, w[0], x[0], start=start, stop=False)
                    mm(o, w[0], x[1], start=False, stop=False)
                    return mm(o, w[1], x[0], start=False, stop=stop)

                def up(j, J):
                    part = slice(GROUP * j, GROUP * (j + 1))
                    h = (hn_hi[:, part], hn_lo[:, part])
                    pe.wait_ge(s_nlo, J + 1)
                    for c, (o, m) in enumerate(CHUNKS):
                        after(pe, s_gu, 3 * (J - 1) + c + 1)
                        for bank, f, semaphore in ((2 * c, HID + o, s_g), (2 * c + 1, o, s_a)):
                            one_pass(ps[0:m, bank, :], (w1_hi[:, f:f + m], w1_lo[:, f:f + m]), h, True, True).then_inc(semaphore, 1)

                def down(j, J):
                    after(pe, s_xf, 2 * J)
                    for c, (o, m) in enumerate(CHUNKS):
                        part = slice(GROUP * c, GROUP * (c + 1))
                        pe.wait_ge(s_glo, 3 * J + c + 1)
                        ins = one_pass(ps[:, 6, :], (w2_hi[0:m, c, :], w2_lo[0:m, c, :]), (gu_hi[0:m, part], gu_lo[0:m, part]),
                                       c == 0, c == len(CHUNKS) - 1)
                    ins.then_inc(s_y2, 1)
                pe.wait_ge(s_w12, 4 * (l + 1))
                def final_transposes(j):
                    if j == GROUPS - 1:
                        pe.wait_ge(s_fs3, 2)
                    else:
                        pe.wait_ge(s_fs, 2 * (j + 1))
                    after(pe, s_fcopy, j)
                    for t in range(4):
                        ins = tr(ps[:, 7, P * t:P * (t + 1)], fin[:, GROUP * j + P * t:GROUP * j + P * (t + 1)], ident[:])
                    ins.then_inc(s_ft, 1)

                for j in range(GROUPS + 1):
                    if j < GROUPS:
                        up(j, GROUPS * l + j)
                    if l == DEPTH - 1 and j == GROUPS:
                        final_transposes(2)
                    if j:
                        down(j - 1, GROUPS * l + j - 1)
                    if l == DEPTH - 1 and 2 <= j < GROUPS:
                        final_transposes(j - 2)
                if l == DEPTH - 1:
                    final_transposes(3)

        @block.scalar
        def _(act):
            act_fn = nc.scalar.activation
            for j in range(GROUPS):
                act.wait_ge(s_xtp, j + 1)
                act_fn(xt[:, GROUP * j:GROUP * (j + 1)], ps[:, j, :], ACT.Copy).then_inc(s_xt, 1)

            def save_v1(j):
                act.wait_ge(s_vp, j + 1)
                act_fn(v1[:, 4 * j:4 * j + 4, :].rearrange("p t d -> p (t d)"), ps[:, 4, :], ACT.Copy).then_inc(s_v, 1)

            def qk_high(j):
                for s, hi in enumerate((qt_hi, kt_hi)):
                    act.wait_ge(s_qkt, 2 * j + s + 1)
                    act_fn(hi[:, GROUP * j:GROUP * (j + 1)], roped[:, s, :], ACT.Copy).then_inc(s_qkh, 1)
            for j in range(2):
                save_v1(j)
                qk_high(j)
            for i in range(TILES + 1):
                if i and i % 4 == 0 and i // 4 + 1 < GROUPS:
                    save_v1(i // 4 + 1)
                if i:
                    for lot in lots_of(i - 1)[:2]:
                        save1(act, lambda o, x: act_fn(o, x, ACT.Copy), lot)
                if i < TILES:
                    act.wait_ge(s_b1, i + 1)
                    if i >= 2:
                        act.wait_ge(s_t1, ends1[i - 2])
                        act.wait_ge(s_ri1, i - 1)
                    act_fn(pbuf[:, i % 2, 0:keys1(i)], ps[:, 0:4, :].rearrange("p b n -> p (b n)")[:, 0:keys1(i)], ACT.Exp,
                           bias=bias[:, i % 2:i % 2 + 1], scale=SCALE1, accum_out=rsum[:, i % 2:i % 2 + 1]).then_inc(s_e1, 1)
                if i and i % 4 == 0 and i // 4 + 1 < GROUPS:
                    qk_high(i // 4 + 1)
            for n, tiles in enumerate((slice(0, 12), slice(12, 16))):
                act.wait_ge(s_ve, n + 1)
                act_fn(std[:, tiles], std[:, tiles], ACT.Sqrt).then_inc(s_sd, 1)
            for j in range(GROUPS):
                act.wait_ge(s_x0p, j + 1)
                act_fn(x0[0:64, GROUP * j:GROUP * (j + 1)], ps[0:64, 4 + j, :], ACT.Copy).then_inc(s_x0a, 1)

            for l in range(DEPTH):
                def project(t, u):
                    T = TILES * l + t
                    qk = qk_all[:, bass.ds(t, 1), :, :].rearrange("p o h d -> p (o h d)")
                    act.wait_ge(s_proj, 3 * T + 1)
                    after(act, s_ss, T - 1)
                    act_fn(sq[:, u, 0:INNER], ps[:, 3 * u, :], ACT.Square).then_inc(s_sq, 1)
                    act_fn(qk[:, 0:INNER], ps[:, 3 * u, :], ACT.Copy).then_inc(s_qs, 1)
                    act.wait_ge(s_proj, 3 * T + 3)
                    after(act, s_vout[u], 8 * (T - u))
                    act_fn(v_tmp[:, u, :], ps[:, 3 * u + 2, :],
                           ACT.Copy).then_inc(s_vsv, 1)
                    act.wait_ge(s_ks, T + 1)
                    act_fn(sq[:, u, INNER:2 * INNER], qk[:, INNER:2 * INNER], ACT.Square).then_inc(s_sq, 1)
                def root(n):
                    tiles = QK_NORM_PARTS[n]
                    act.wait_ge(s_nm, 2 * l + n + 1)
                    act_fn(ssm[:, tiles], ssm[:, tiles], ACT.Sqrt).then_inc(s_nq, 1)
                tiles_in_pairs(act, 0, 2, TILES - 2, TILES - 2, project)
                root(0)
                project(TILES - 2, 0)
                project(TILES - 1, 1)
                root(1)

                def transposed(t, T, u):
                    act.wait_ge(s_tt, 2 * T + 1)
                    act_fn(kring[:, :, u:u + 3:2, :], ps[:, 0, :].rearrange("p (g a k) -> p g a k", g=PAIRS, a=2),
                           ACT.Copy).then_inc(s_kev, 1)
                    act.wait_ge(s_tt, 2 * T + 2)
                    for h, (a, b) in enumerate(HALVES):
                        ins = act_fn(qbd[a:b, :, :, h, :], ps[a:b, 1, :].rearrange("p (g w q) -> p g w q", g=PAIRS, w=2), ACT.Copy)
                        if h:
                            ins.then_inc(s_qev, 1)

                def exponentials(t, T, u):
                    after(act, s_pn, T - 1)
                    after(act, s_inv, T)
                    for c in range(8):
                        if c % 4 == 0:
                            act.wait_ge(s_mx, 2 * T + c // 4 + 1)
                        act_fn(sc[u][:, P * c:P * (c + 1)], ps[:, 2 + c // 4, P * (c % 4):P * (c % 4 + 1)], ACT.Exp,
                               bias=smax[:, c:c + 1], accum_out=ssum[:, c:c + 1]).then_inc(s_exp, 1)

                def save_pt(t, T, u):
                    after(act, s_pv, T)
                    for b in range(2):
                        act.wait_ge(s_pt, 2 * T + b + 1)
                        act_fn(pt2[:, 512 * b:512 * (b + 1)], ps[:, 4 + b, :], ACT.Copy).then_inc(s_pte, 1)

                def save_centred(n):
                    _, a, b = FFN_NORM_PARTS[n]
                    act.wait_ge(s_cp, len(FFN_NORM_PARTS) * l + n + 1)
                    act_fn(sqf[:, P * a:P * b], norm_part(n), ACT.Square).then_inc(s_sqf, 1)
                    act_fn(hc[:, P * a:P * b], norm_part(n), ACT.Copy).then_inc(s_hc, 1)

                def variance_log(n):
                    _, a, b = FFN_NORM_PARTS[n]
                    act.wait_ge(s_vp2, len(FFN_NORM_PARTS) * l + n + 1)
                    act_fn(rs[:, P * a:P * b], norm_part(n), ACT.Ln, bias=eps[:, 0:1]).then_inc(s_ln, 1)

                def step(t, u):
                    T = TILES * l + t
                    exact = isinstance(t, int)
                    if not (exact and not 0 <= t < TILES):
                        exponentials(t, T, u)
                    if not (exact and t + 1 >= TILES):
                        transposed(t + 1, T + 1, 1 - u)
                    if exact and t == TILES:
                        save_centred(0)
                    if not (exact and t < 1):
                        save_pt(t - 1, T - 1, 1 - u)
                    if exact and t == TILES:
                        save_centred(1)
                        save_centred(2)
                tiles_in_pairs(act, -1, 2, TILES - 2, TILES + 1, step)

                def hn_high(j):
                    part = slice(GROUP * j, GROUP * (j + 1))
                    act.wait_ge(s_hn, GROUPS * l + j + 1)
                    act_fn(hn_hi[:, part], hn[:, part], ACT.Copy).then_inc(s_nhi, 1)

                def gelu(J, c):
                    m = CHUNKS[c][1]
                    act.wait_ge(s_g, 3 * J + c + 1)
                    act_fn(ge[0:m, GROUP * c:GROUP * (c + 1)], ps[0:m, 2 * c, :], ACT.Gelu,
                           bias=b1[0:m, l, 1, c:c + 1]).then_inc(s_ge, 1)

                def gated_high(J, c):
                    m, part = CHUNKS[c][1], slice(GROUP * c, GROUP * (c + 1))
                    act.wait_ge(s_gu, 3 * J + c + 1)
                    after(act, s_y2, J)
                    act_fn(gu_hi[0:m, part], gu[0:m, part], ACT.Copy).then_inc(s_ghi, 1)
                def final_copy(j):
                    act.wait_ge(s_ft, j + 1)
                    act_fn(y_out[:, 4 * j:4 * j + 4, :].rearrange("p t d -> p (t d)"), ps[:, 7, :], ACT.Copy).then_inc(s_fcopy, 1)

                for j in range(3):
                    variance_log(j)
                save_centred(3)
                save_centred(4)
                variance_log(3)
                variance_log(4)
                for j in range(GROUPS):
                    part = slice(GROUP * j, GROUP * (j + 1))
                    act.wait_ge(s_ln, len(FFN_NORM_PARTS) * l + (j + 1 if j < 3 else 5))
                    act_fn(rs[:, part], rs[:, part], ACT.Exp, scale=-0.5).then_inc(s_rs, 1)
                hn_high(0)
                for j in range(GROUPS):
                    J = GROUPS * l + j
                    if j + 1 < GROUPS:
                        hn_high(j + 1)
                    gelu(J, 0)
                    gelu(J, 1)
                    if j == GROUPS - 1:
                        gelu(J, 2)
                    gated_high(J, 0)
                    if j < GROUPS - 1:
                        gelu(J, 2)
                    gated_high(J, 1)
                    gated_high(J, 2)
                    if l == DEPTH - 1 and j >= 2:
                        final_copy(j - 2)
                if l == DEPTH - 1:
                    final_copy(2)
                    act.wait_ge(s_ve, 3)
                    act_fn(std[:, 0:12], std[:, 0:12], ACT.Sqrt).then_inc(s_sd, 1)
            act.wait_ge(s_ve, 4)
            act_fn(std[:, 12:16], std[:, 12:16], ACT.Sqrt).then_inc(s_sd, 1)

        @block.vector
        def _(dve):
            v = nc.vector
            v.memset(eps[:], EPS).then_inc(s_eps, 1)

            def rope1_chunk(j):
                part = slice(GROUP * j, GROUP * (j + 1))
                dve.wait_ge(s_rope[j], 16)
                for s in range(2):
                    n = 2 * j + s
                    dve.wait_ge(s_qkp, n + 1)
                    after(dve, s_qkt, n)
                    for r in range(2):
                        v.tensor_tensor(rope_tmp[:, r, :], ps[:, 4 + 2 * s + r, :], rope[:, r, part],
                                        ALU.mult).then_inc(s_rsn if r else s_rc, 1)
                    dve.wait_ge(s_rc, n + 1)
                    dve.wait_ge(s_rsn, n + 1)
                    after(dve, s_qkl, n - 1)
                    v.tensor_tensor(roped[:, s, :], rope_tmp[:, 0, :], rope_tmp[:, 1, :], ALU.add).then_inc(s_qkt, 1)

            def maximum1(i):
                dve.wait_ge(s_s1, i + 1)
                after(dve, s_e1, i - 1)
                v.tensor_reduce(nmax[:, i % 2:i % 2 + 1], ps[:, 0:4, :].rearrange("p b n -> p (b n)")[:, 0:keys1(i)],
                                AX.X, ALU.max, negate=True).then_inc(s_m1, 1)
                dve.wait_ge(s_m1, i + 1)
                v.tensor_scalar(bias[:, i % 2:i % 2 + 1], nmax[:, i % 2:i % 2 + 1], SCALE1, None, ALU.mult).then_inc(s_b1, 1)

            def residual1(i):
                v.reciprocal(rinv[:, i % 2:i % 2 + 1], rsum[:, i % 2:i % 2 + 1]).then_inc(s_ri1, 1)
                dve.wait_ge(s_ri1, i + 1)
                dve.wait_ge(s_pv1, ends1[i])
                v.scalar_tensor_tensor(x_tok[:, i, :], ps[:, 6 + i % 2, 0:P], rinv[:, i % 2:i % 2 + 1], x_tok[:, i, :],
                                       ALU.mult, ALU.add).then_inc(s_o1, 1)
                dve.wait_ge(s_o1, i + 1)
                v.bn_stats(stats[:, i, :], x_tok[:, i, :]).then_inc(s_bs, 1)
                dve.wait_ge(s_bs, i + 1)
                v.bn_aggr(mean_var[:, i, :], stats[:, i, :]).then_inc(s_ba, 1)

            def inverse_std(n, tiles):
                var_eps(n, tiles)
                invert_std(n, tiles)

            def var_eps(n, tiles):
                dve.wait_ge(s_ba, TILES * (n // 2) + tiles.stop)
                v.tensor_scalar(std[:, tiles], mean_var[:, tiles, 1], EPS, None, ALU.add).then_inc(s_ve, 1)

            def invert_std(n, tiles):
                dve.wait_ge(s_sd, n + 1)
                v.reciprocal(rstd[:, tiles], std[:, tiles]).then_inc(s_rd, 1)
                dve.wait_ge(s_rd, n + 1)

            def normalise1(t):
                v.tensor_scalar(x_tok[:, t, :], x_tok[:, t, :], mean_var[:, t, 0:1], rstd[:, t:t + 1],
                                ALU.subtract, ALU.mult).then_inc(s_ln1, 1)

            def save_x0(j):
                dve.wait_ge(s_x0p, j + 1)
                v.tensor_copy(x0[64:128, GROUP * j + 1:GROUP * (j + 1) + 1], ps[64:128, 4 + j, :]).then_inc(s_x0v, 1)
            for j in range(2):
                rope1_chunk(j)
            for i in range(TILES + 1):
                if i and i % 4 == 0 and i // 4 + 1 < GROUPS:
                    rope1_chunk(i // 4 + 1)
                if i < TILES:
                    maximum1(i)
                if i == TILES:
                    var_eps(0, slice(0, 12))
                if i:
                    for lot in lots_of(i - 1)[2:]:
                        save1(dve, v.tensor_copy, lot)
                if i == TILES:
                    invert_std(0, slice(0, 12))
                    for t in range(4):
                        normalise1(t)
                if i:
                    dve.wait_ge(s_e1, i)
                    residual1(i - 1)
            var_eps(1, slice(12, 16))
            for t in range(4, 8):
                normalise1(t)
            save_x0(0)
            for t in range(8, 12):
                normalise1(t)
            invert_std(1, slice(12, 16))
            for t in range(12, 16):
                normalise1(t)
            for j in range(1, GROUPS):
                save_x0(j)

            def final_tile(t):
                return ps[:, 7, P * (t % 4):P * (t % 4 + 1)] if t >= 12 else y_out[:, t, :]

            def final_stats(j):
                if j == 3:
                    dve.wait_ge(s_ft, j + 1)
                else:
                    dve.wait_ge(s_fcopy, j + 1)
                for t in range(4 * j, 4 * j + 4):
                    v.bn_stats(stats[:, t, :], final_tile(t)).then_inc(s_bs, 1)
                for t in range(4 * j, 4 * j + 4):
                    dve.wait_ge(s_bs, TILES + t + 1)
                    v.bn_aggr(mean_var[:, t, :], stats[:, t, :]).then_inc(s_ba, 1)

            def final_norm(t):
                v.tensor_scalar(y_out[:, t, :], final_tile(t), mean_var[:, t, 0:1], rstd[:, t:t + 1],
                                ALU.subtract, ALU.mult).then_inc(s_fo, 1)

            def stage_low(l, t, u):
                T = TILES * l + t
                src = xa if l else x0
                if l == 0 and isinstance(t, int) and t == 2:
                    dve.wait_ge(s_x0a, GROUPS)
                    dve.wait_ge(s_x0v, GROUPS)
                dve.wait_ge(s_hs, T + 1)
                after(dve, s_proj, 3 * (T - 1))
                v.tensor_tensor(hs_lo[:, u, :], src[:, bass.ds(P * t, P)], hs_hi[:, u, :].bitcast(F), ALU.subtract).then_inc(s_hl, 1)

            for l in range(DEPTH):
                src = xa if l else x0

                def save_k(t, u):
                    T = TILES * l + t
                    dve.wait_ge(s_proj, 3 * T + 2)
                    v.tensor_copy(qk_all[:, bass.ds(t, 1), HEADS:2 * HEADS, :].rearrange("p o h d -> p (o h d)"),
                                  ps[:, 3 * u + 1, :]).then_inc(s_ks, 1)

                def project(t, u):
                    if l and isinstance(t, int) and t == 1:
                        dve.wait_ge(s_xf, 2 * GROUPS * l)
                    if not (isinstance(t, int) and t + 1 >= TILES) and not (l and isinstance(t, int) and t == 0):
                        stage_low(l, t + 1, 1 - u)
                    save_k(t, u)
                    if not (isinstance(t, int) and t == 0):
                        sum_squares(t - 1, 1 - u)

                def sum_squares(t, u):
                    T = TILES * l + t
                    dve.wait_ge(s_sq, 2 * T + 2)
                    v.tensor_reduce(ss[:, bass.ds(t, 1), :].rearrange("p o h -> p (o h)"), sq[:, u, :].rearrange("p (h d) -> p h d", d=DH),
                                    AX.X, ALU.add).then_inc(s_ss, 1)
                if l == 0:
                    dve.wait_ge(s_x0a, 1)
                    dve.wait_ge(s_x0v, 1)
                    stage_low(0, 0, 0)
                def clip(n):
                    tiles = QK_NORM_PARTS[n]
                    dve.wait_ge(s_ss, TILES * l + tiles.stop)
                    v.tensor_scalar(ssm[:, tiles], ss[:, tiles], 1e-24, None, ALU.max).then_inc(s_nm, 1)

                def invert_norm(n):
                    tiles = QK_NORM_PARTS[n]
                    dve.wait_ge(s_nq, 2 * l + n + 1)
                    v.reciprocal(rn[:, tiles], ssm[:, tiles]).then_inc(s_nr, 1)
                    dve.wait_ge(s_nr, 2 * l + n + 1)
                tiles_in_pairs(dve, 0, 2, TILES - 2, TILES - 2, project)
                clip(0)
                project(TILES - 2, 0)
                invert_norm(0)

                def normalise(t, T):
                    after(dve, s_tc, T)
                    after(dve, s_ts, 2 * T)
                    v.tensor_tensor(qn, qk_all[:, bass.ds(t, 1), :, :].rearrange("p o h d -> p (o h) d"),
                                    rn[:, bass.ds(t, 1), :].rearrange("p o h -> p (o h)")[:, :, None].to_broadcast([P, 2 * HEADS, DH]),
                                    ALU.mult).then_inc(s_qn, 1)

                def times_sin(t, T):
                    dve.wait_ge(s_scaled, 3 * T + 3)
                    dve.wait_ge(s_qn, T + 1)
                    after(dve, s_qr, T)
                    qh, th = (z.rearrange("p (s h) d -> p s h d", s=2) for z in (qn, ts))
                    for h in range(2):
                        o, i = slice(32 * h, 32 * h + 32), slice(32 * (1 - h), 32 * (1 - h) + 32)
                        v.tensor_tensor(th[:, :, :, o], qh[:, :, :, i],
                                        scaled[:, 1, :, bass.ds(t, 1), o].to_broadcast([P, 2, HEADS, 32]),
                                        ALU.mult).then_inc(s_ts, 1)

                def rotate(t, T):
                    dve.wait_ge(s_ts, 2 * T + 2)
                    dve.wait_ge(s_tc, T + 1)
                    v.tensor_tensor(qr, tc.rearrange("p h d -> p (h d)"), ts.rearrange("p h d -> p (h d)"), ALU.add).then_inc(s_qr, 1)

                def maximum(t, T, u):
                    for b in range(2):
                        dve.wait_ge(s_s, 2 * T + b + 1)
                        v.tensor_reduce(smax[:, 4 * b:4 * b + 4], ps[:, 2 + b, :].rearrange("p (c k) -> p c k", c=4),
                                        AX.X, ALU.max, negate=True).then_inc(s_mx, 1)

                def invert_sums(t, T, u):
                    dve.wait_ge(s_exp, 8 * T + 8)
                    after(dve, s_pn, T)
                    v.reciprocal(sinv[:], ssum[:]).then_inc(s_inv, 1)

                def save_out(t, T, u):
                    dve.wait_ge(s_pv, T + 1)
                    after(dve, s_y, T)
                    for h, (a, b) in enumerate(HALVES):
                        o = ps[a:b, 6:8, :].rearrange("p b (g w h q) -> p (b g w) h q", g=2, w=2, h=2)
                        v.tensor_copy(ot[a:b].rearrange("p g (w q) -> p (g w) q", w=2), o[:, :, h, :]).then_inc(s_oe, 1)

                def residual(t, T):
                    dve.wait_ge(s_y, T + 1)
                    for h, (a, b) in enumerate(HALVES):
                        c = bass.ds(P * t + h, P)
                        v.tensor_tensor(xb[a:b, c], ps[a:b, 0, 0:P], src[a:b, c], ALU.add).then_inc(s_xb, 1)

                def step(t, u):
                    T = TILES * l + t
                    exact = isinstance(t, int)
                    ahead = not (exact and t + 2 >= TILES)
                    now = not (exact and not 0 <= t < TILES)
                    behind = not (exact and t < 2)
                    if now and not (exact and t == 0):
                        maximum(t, T, u)
                    if ahead:
                        normalise(t + 2, T + 2)
                    if behind:
                        save_out(t - 2, T - 2, u)
                    if ahead:
                        times_sin(t + 2, T + 2)
                    if now:
                        invert_sums(t, T, u)
                    if behind:
                        residual(t - 2, T - 2)
                    if ahead:
                        rotate(t + 2, T + 2)
                T = TILES * l
                normalise(0, T)
                save_k(TILES - 1, 1)
                times_sin(0, T)
                sum_squares(TILES - 2, 0)
                rotate(0, T)
                sum_squares(TILES - 1, 1)
                clip(1)
                normalise(1, T + 1)
                invert_norm(1)
                times_sin(1, T + 1)
                maximum(0, T, 0)
                rotate(1, T + 1)
                tiles_in_pairs(dve, 0, 2, TILES - 2, TILES + 2, step)

                dve.wait_ge(s_wrest, 16 * 28)
                for j in range(GROUPS):
                    J = GROUPS * l + j
                    part = slice(GROUP * j, GROUP * (j + 1))
                    dve.wait_ge(s_hc, len(FFN_NORM_PARTS) * l + (j + 1 if j < 3 else 5))
                    dve.wait_ge(s_rs, J + 1)
                    v.tensor_tensor(hn[:, part], hc[:, part], rs[:, part], ALU.mult).then_inc(s_hr, 1)
                    dve.wait_ge(s_hr, J + 1)
                    v.tensor_scalar(hn[:, part], hn[:, part], cols[:, l, 0:1], cols[:, l, 1:2], ALU.mult, ALU.add).then_inc(s_hn, 1)
                def gate(J, c):
                    m, part = CHUNKS[c][1], slice(GROUP * c, GROUP * (c + 1))
                    dve.wait_ge(s_a, 3 * J + c + 1)
                    dve.wait_ge(s_ge, 3 * J + c + 1)
                    after(dve, s_ghi, 3 * (J - 1) + c + 1)
                    after(dve, s_glo, 3 * (J - 1) + c + 1)
                    v.scalar_tensor_tensor(gu[0:m, part], ps[0:m, 2 * c + 1, :], b1[0:m, l, 0, c:c + 1],
                                           ge[0:m, part], ALU.add, ALU.mult).then_inc(s_gu, 1)

                def gated_low(J):
                    after(dve, s_y2, J)
                    for c, (o, m) in enumerate(CHUNKS):
                        part = slice(GROUP * c, GROUP * (c + 1))
                        dve.wait_ge(s_ghi, 3 * J + c + 1)
                        v.tensor_tensor(gu_lo[0:m, part], gu[0:m, part], gu_hi[0:m, part].bitcast(F), ALU.subtract).then_inc(s_glo, 1)

                def residual2(j, J):
                    dve.wait_ge(s_y2, J + 1)
                    for h, (a, b) in enumerate(HALVES):
                        part = slice(GROUP * j + h, GROUP * (j + 1) + h)
                        v.scalar_tensor_tensor(xa[a:b, part], ps[a:b, 6, :], cols[a:b, l, 2:3], xb[a:b, part],
                                               ALU.add, ALU.add).then_inc(s_xf, 1)
                for j in range(GROUPS):
                    J = GROUPS * l + j
                    gate(J, 0)
                    gate(J, 1)
                    if j < GROUPS - 1:
                        gate(J, 2)
                    if j:
                        residual2(j - 1, J - 1)
                    if j == GROUPS - 1:
                        gate(J, 2)
                    gated_low(J)
                    if l == DEPTH - 1 and j >= 2:
                        final_stats(j - 2)
                if l == DEPTH - 1:
                    final_stats(2)
                    inverse_std(2, slice(0, 12))
                else:
                    dve.wait_ge(s_xf, 2 * (GROUPS * l + 1))
                    for t in range(2):
                        stage_low(l + 1, t, t)
                residual2(GROUPS - 1, GROUPS * (l + 1) - 1)
            dve.wait_ge(s_xf, 2 * GROUPS * DEPTH)
            for h, (a, b) in enumerate(HALVES):
                part = slice(GROUP * 3 + h, GROUP * 4 + h)
                v.tensor_tensor(fin[a:b, GROUP * 3:GROUP * 4], xa[a:b, part], x0[a:b, part], ALU.add).then_inc(s_fs3, 1)
            for t in range(4):
                final_norm(t)
            final_stats(3)
            var_eps(3, slice(12, 16))
            for t in range(4, 12):
                final_norm(t)
            invert_std(3, slice(12, 16))
            for t in range(12, 16):
                final_norm(t)


def rope_constants():
    i = np.arange(D // 2, dtype=np.float32)
    theta = np.power(np.float32(10000.0), (np.float32(-2.0) * i / np.float32(D)).astype(np.float32)).astype(np.float32)
    angle = np.arange(N, dtype=np.float32)[:, None] * theta[None, :]
    cos, sin = np.cos(angle).astype(np.float32), np.sin(angle).astype(np.float32)
    sign = np.where(np.arange(D) % 2 == 0, -1.0, 1.0).astype(np.float32)
    return np.ascontiguousarray(np.stack([np.repeat(cos, 2, 1).T, (np.repeat(sin, 2, 1) * sign).T]))


def xpos_constants():
    f = np.float32
    half = np.arange(0, DH, 2, dtype=f)
    inv = (f(1.0) / np.power(f(10000.0), half / f(DH))).astype(f)
    t = np.arange(N, dtype=f)
    freqs = t[:, None] * inv[None, :]
    base = (half + f(0.4 * DH)) / f(1.4 * DH)
    power = (t - f(N // 2)) / f(WINDOW // 2)
    scale = np.power(base[None, :], power[:, None]).astype(f)
    both = lambda a: np.concatenate([a, a], -1).astype(f)
    cos, sin, scale = both(np.cos(freqs)), both(np.sin(freqs)), both(scale)
    sign = np.where(np.arange(DH) < DH // 2, -1.0, 1.0).astype(f)
    of_cos, of_sin = [cos * scale * f(8), cos / scale], [sin * scale * sign * f(8), sin / scale * sign]
    return np.ascontiguousarray(np.stack([np.stack(of_cos), np.stack(of_sin)]))


def kernel(L0_attn_x, L0_attn_Wq, L0_attn_Wk, L0_attn_Wv, L0_ffn_wqkv, L0_ffn_q_scale, L0_ffn_k_scale, L0_ffn_wo,
           L0_ffn_ln_g, L0_ffn_ln_b, L0_ffn_w1, L0_ffn_b1, L0_ffn_w2, L0_ffn_b2):
    import concourse.bacc as bacc
    from concourse.bass_utils import run_bass_kernel_spmd

    swap = np.arange(D) ^ 1
    wq, wk, wv = (np.asarray(w).T for w in (L0_attn_Wq, L0_attn_Wk, L0_attn_Wv))
    arrays = {
        "x": L0_attn_x,
        "w_qkv1": np.stack([wq, wq[:, swap], wk, wk[:, swap], wv]),
        "rope1": rope_constants(),
        "w_qkv": L0_ffn_wqkv, "q_scale": L0_ffn_q_scale, "k_scale": L0_ffn_k_scale, "w_o": L0_ffn_wo,
        "ln_g": L0_ffn_ln_g, "ln_b": L0_ffn_ln_b, "w_1": L0_ffn_w1, "b_1": L0_ffn_b1, "w_2": L0_ffn_w2, "b_2": L0_ffn_b2,
        "xpos": xpos_constants(),
    }
    nc = bacc.Bacc("TRN2", target_bir_lowering=False, num_devices=1)
    feeds, args = {}, []
    for name, a in arrays.items():
        a = np.ascontiguousarray(np.asarray(a))
        feeds[f"in_{name}"] = a
        args.append(nc.dram_tensor(f"in_{name}", a.shape, mybir.dt.from_np(a.dtype), kind="ExternalInput").ap())
    out = nc.dram_tensor("out", (1, N, D), mybir.dt.float32, kind="ExternalOutput").ap()
    build(nc, *args, out)
    r = run_bass_kernel_spmd(nc, [feeds], core_ids=[0])
    return r.results[0]["out"]
```
